# Optimizing a Trainium2 kernel written in Bass

```python
import numpy as np
import jax
import jax.numpy as jnp

def _softmax(x, axis=-1):
    return jax.nn.softmax(x, axis=axis)

def _gelu(x):
    return jax.nn.gelu(x, approximate=True)

def _silu(x):
    return jax.nn.silu(x)

def _sigmoid(x):
    return jax.nn.sigmoid(x)

def _layernorm(x, axis=-1, eps=1e-05):
    m = jnp.mean(x, axis=axis, keepdims=True)
    v = jnp.var(x, axis=axis, keepdims=True)
    return (x - m) / jnp.sqrt(v + eps)

def _scatter_add(tgt, idx, src, axis=0):
    return tgt.at[idx].add(src)

def _segment_sum(src, seg, n):
    return jax.ops.segment_sum(src, seg, n)
kernel_name = 'mk_dlrm_tower_d1_rec_r8_059f27'

def setup_inputs(seed: int=0):
    np.random.seed(seed)
    _w = jnp.asarray

    def _rec_inputs():
        import jax
        import jax.numpy as jnp
        _tk = jax.random.key(seed)
        dense_ctx = jax.random.normal(jax.random.fold_in(_tk, 190), (2048, 16), jnp.float32)
        ids = jnp.stack([jax.random.randint(jax.random.fold_in(_tk, 200 + f), (2048,), 0, v, jnp.int32) for f, v in enumerate([12500, 1000, 1250, 1250, 1250, 1000, 12500, 1250, 12500, 1250, 12500, 12500, 12500, 125000, 12500, 125000, 1000, 12500, 125000, 12500, 125000, 1250, 1250, 125000, 1250, 1250])], axis=1)
        tbl_0 = 0.05 * jax.random.normal(jax.random.fold_in(_tk, 500 + 0), (12500, 32), jnp.float32)
        tbl_1 = 0.05 * jax.random.normal(jax.random.fold_in(_tk, 500 + 1), (1000, 32), jnp.float32)
        tbl_2 = 0.05 * jax.random.normal(jax.random.fold_in(_tk, 500 + 2), (1250, 32), jnp.float32)
        tbl_3 = 0.05 * jax.random.normal(jax.random.fold_in(_tk, 500 + 3), (1250, 32), jnp.float32)
        tbl_4 = 0.05 * jax.random.normal(jax.random.fold_in(_tk, 500 + 4), (1250, 32), jnp.float32)
        tbl_5 = 0.05 * jax.random.normal(jax.random.fold_in(_tk, 500 + 5), (1000, 32), jnp.float32)
        tbl_6 = 0.05 * jax.random.normal(jax.random.fold_in(_tk, 500 + 6), (12500, 32), jnp.float32)
        tbl_7 = 0.05 * jax.random.normal(jax.random.fold_in(_tk, 500 + 7), (1250, 32), jnp.float32)
        tbl_8 = 0.05 * jax.random.normal(jax.random.fold_in(_tk, 500 + 8), (12500, 32), jnp.float32)
        tbl_9 = 0.05 * jax.random.normal(jax.random.fold_in(_tk, 500 + 9), (1250, 32), jnp.float32)
        tbl_10 = 0.05 * jax.random.normal(jax.random.fold_in(_tk, 500 + 10), (12500, 32), jnp.float32)
        tbl_11 = 0.05 * jax.random.normal(jax.random.fold_in(_tk, 500 + 11), (12500, 32), jnp.float32)
        tbl_12 = 0.05 * jax.random.normal(jax.random.fold_in(_tk, 500 + 12), (12500, 32), jnp.float32)
        tbl_13 = 0.05 * jax.random.normal(jax.random.fold_in(_tk, 500 + 13), (125000, 32), jnp.float32)
        tbl_14 = 0.05 * jax.random.normal(jax.random.fold_in(_tk, 500 + 14), (12500, 32), jnp.float32)
        tbl_15 = 0.05 * jax.random.normal(jax.random.fold_in(_tk, 500 + 15), (125000, 32), jnp.float32)
        tbl_16 = 0.05 * jax.random.normal(jax.random.fold_in(_tk, 500 + 16), (1000, 32), jnp.float32)
        tbl_17 = 0.05 * jax.random.normal(jax.random.fold_in(_tk, 500 + 17), (12500, 32), jnp.float32)
        tbl_18 = 0.05 * jax.random.normal(jax.random.fold_in(_tk, 500 + 18), (125000, 32), jnp.float32)
        tbl_19 = 0.05 * jax.random.normal(jax.random.fold_in(_tk, 500 + 19), (12500, 32), jnp.float32)
        tbl_20 = 0.05 * jax.random.normal(jax.random.fold_in(_tk, 500 + 20), (125000, 32), jnp.float32)
        tbl_21 = 0.05 * jax.random.normal(jax.random.fold_in(_tk, 500 + 21), (1250, 32), jnp.float32)
        tbl_22 = 0.05 * jax.random.normal(jax.random.fold_in(_tk, 500 + 22), (1250, 32), jnp.float32)
        tbl_23 = 0.05 * jax.random.normal(jax.random.fold_in(_tk, 500 + 23), (125000, 32), jnp.float32)
        tbl_24 = 0.05 * jax.random.normal(jax.random.fold_in(_tk, 500 + 24), (1250, 32), jnp.float32)
        tbl_25 = 0.05 * jax.random.normal(jax.random.fold_in(_tk, 500 + 25), (1250, 32), jnp.float32)
        _rk = jax.random.fold_in(_tk, 7)
        W_top1 = 0.0606339 * jax.random.normal(jax.random.fold_in(_tk, 801), (272, 512), jnp.float32)
        W_top2 = 0.0441942 * jax.random.normal(jax.random.fold_in(_tk, 802), (512, 256), jnp.float32)
        W_top3 = 0.0625 * jax.random.normal(jax.random.fold_in(_tk, 803), (256, 1), jnp.float32)
        b_top1 = jnp.zeros((512,), jnp.float32)
        b_top2 = jnp.zeros((256,), jnp.float32)
        return (dense_ctx, ids, tbl_0, tbl_1, tbl_2, tbl_3, tbl_4, tbl_5, tbl_6, tbl_7, tbl_8, tbl_9, tbl_10, tbl_11, tbl_12, tbl_13, tbl_14, tbl_15, tbl_16, tbl_17, tbl_18, tbl_19, tbl_20, tbl_21, tbl_22, tbl_23, tbl_24, tbl_25, W_top1, b_top1, W_top2, b_top2, W_top3)
    dense_ctx, ids, tbl_0, tbl_1, tbl_2, tbl_3, tbl_4, tbl_5, tbl_6, tbl_7, tbl_8, tbl_9, tbl_10, tbl_11, tbl_12, tbl_13, tbl_14, tbl_15, tbl_16, tbl_17, tbl_18, tbl_19, tbl_20, tbl_21, tbl_22, tbl_23, tbl_24, tbl_25, W_top1, b_top1, W_top2, b_top2, W_top3 = _rec_inputs()

    def _L0_rec_setup():
        import jax, jax.numpy as jnp
        import numpy as np
        M_FIELDS = 26
        H1 = 128
        H2 = 128
        BATCH = 256
        EMB_K = 32

        def _cin_layer(x_prev, x0, W, b):
            return jnp.einsum('bik,bjk,hij->bhk', x_prev, x0, W) + b[None, :, None]
        key = jax.random.key(seed)
        k0, k1, k2, k3, k4 = jax.random.split(key, 5)
        inputs = jax.random.normal(k0, (BATCH, M_FIELDS, EMB_K), dtype=jnp.float32)
        W1 = jax.random.normal(k1, (H1, M_FIELDS, M_FIELDS), dtype=jnp.float32) * 0.05
        b1 = jax.random.normal(k2, (H1,), dtype=jnp.float32) * 0.05
        W2 = jax.random.normal(k3, (H2, H1, M_FIELDS), dtype=jnp.float32) * 0.05
        b2 = jax.random.normal(k4, (H2,), dtype=jnp.float32) * 0.05
        return {'inputs': inputs, 'W1': W1, 'b1': b1, 'W2': W2, 'b2': b2}
    _L0_rec_all = _L0_rec_setup()
    _L0_rec_in = {k: v for k, v in _L0_rec_all.items() if k in ('W1', 'b1', 'W2', 'b2')}
    del _L0_rec_all
    return {'dense_ctx': dense_ctx, 'ids': ids, 'tbl_0': tbl_0, 'tbl_1': tbl_1, 'tbl_2': tbl_2, 'tbl_3': tbl_3, 'tbl_4': tbl_4, 'tbl_5': tbl_5, 'tbl_6': tbl_6, 'tbl_7': tbl_7, 'tbl_8': tbl_8, 'tbl_9': tbl_9, 'tbl_10': tbl_10, 'tbl_11': tbl_11, 'tbl_12': tbl_12, 'tbl_13': tbl_13, 'tbl_14': tbl_14, 'tbl_15': tbl_15, 'tbl_16': tbl_16, 'tbl_17': tbl_17, 'tbl_18': tbl_18, 'tbl_19': tbl_19, 'tbl_20': tbl_20, 'tbl_21': tbl_21, 'tbl_22': tbl_22, 'tbl_23': tbl_23, 'tbl_24': tbl_24, 'tbl_25': tbl_25, 'W_top1': W_top1, 'b_top1': b_top1, 'W_top2': W_top2, 'b_top2': b_top2, 'W_top3': W_top3, 'L0_rec_W1': _L0_rec_in['W1'], 'L0_rec_b1': _L0_rec_in['b1'], 'L0_rec_W2': _L0_rec_in['W2'], 'L0_rec_b2': _L0_rec_in['b2']}

def reference(dense_ctx, ids, tbl_0, tbl_1, tbl_2, tbl_3, tbl_4, tbl_5, tbl_6, tbl_7, tbl_8, tbl_9, tbl_10, tbl_11, tbl_12, tbl_13, tbl_14, tbl_15, tbl_16, tbl_17, tbl_18, tbl_19, tbl_20, tbl_21, tbl_22, tbl_23, tbl_24, tbl_25, W_top1, b_top1, W_top2, b_top2, W_top3, L0_rec_W1, L0_rec_b1, L0_rec_W2, L0_rec_b2):
    import jax
    import jax.numpy as jnp

    def _L0_rec_ref(inputs, W1, b1, W2, b2):
        import jax, jax.numpy as jnp
        import numpy as np
        M_FIELDS = 26
        H1 = 128
        H2 = 128
        BATCH = 256
        EMB_K = 32

        def _cin_layer(x_prev, x0, W, b):
            return jnp.einsum('bik,bjk,hij->bhk', x_prev, x0, W) + b[None, :, None]
        x1 = _cin_layer(inputs, inputs, W1, b1)
        x2 = _cin_layer(x1, inputs, W2, b2)
        res = jnp.concatenate([x1, x2], axis=1)
        return jnp.sum(res, axis=-1)
    e = jnp.stack([tbl_0[ids[:, 0]], tbl_1[ids[:, 1]], tbl_2[ids[:, 2]], tbl_3[ids[:, 3]], tbl_4[ids[:, 4]], tbl_5[ids[:, 5]], tbl_6[ids[:, 6]], tbl_7[ids[:, 7]], tbl_8[ids[:, 8]], tbl_9[ids[:, 9]], tbl_10[ids[:, 10]], tbl_11[ids[:, 11]], tbl_12[ids[:, 12]], tbl_13[ids[:, 13]], tbl_14[ids[:, 14]], tbl_15[ids[:, 15]], tbl_16[ids[:, 16]], tbl_17[ids[:, 17]], tbl_18[ids[:, 18]], tbl_19[ids[:, 19]], tbl_20[ids[:, 20]], tbl_21[ids[:, 21]], tbl_22[ids[:, 22]], tbl_23[ids[:, 23]], tbl_24[ids[:, 24]], tbl_25[ids[:, 25]]], axis=1)
    z = _L0_rec_ref(e, L0_rec_W1, L0_rec_b1, L0_rec_W2, L0_rec_b2)
    z = z.reshape(z.shape[0], -1)
    h = jnp.concatenate([z, dense_ctx], axis=1)
    h = jnp.maximum(h @ W_top1 + b_top1, 0.0)
    h = jnp.maximum(h @ W_top2 + b_top2, 0.0)
    y = h @ W_top3
    return y

_drawn_inputs = setup_inputs


def setup_inputs(seed=0):
    import zlib

    import numpy as np

    out = dict(_drawn_inputs(seed))
    spreads = {'b_top1': (0.0, 2.0), 'b_top2': (0.0, 0.8)}
    factors = {'tbl_0': 8.0,
     'tbl_1': 8.0,
     'tbl_2': 8.0,
     'tbl_3': 8.0,
     'tbl_4': 8.0,
     'tbl_5': 8.0,
     'tbl_6': 8.0,
     'tbl_7': 8.0,
     'tbl_8': 8.0,
     'tbl_9': 8.0,
     'tbl_10': 8.0,
     'tbl_11': 8.0,
     'tbl_12': 8.0,
     'tbl_13': 8.0,
     'tbl_14': 8.0,
     'tbl_15': 8.0,
     'tbl_16': 8.0,
     'tbl_17': 8.0,
     'tbl_18': 8.0,
     'tbl_19': 8.0,
     'tbl_20': 8.0,
     'tbl_21': 8.0,
     'tbl_22': 8.0,
     'tbl_23': 8.0,
     'tbl_24': 8.0,
     'tbl_25': 8.0,
     'L0_rec_W1': 8.0,
     'L0_rec_W2': 4.227,
     'dense_ctx': 6.219}
    for name, (base, spread) in spreads.items():
        noise = np.random.default_rng([zlib.crc32(name.encode()), seed]).standard_normal(out[name].shape)
        drawn = base * np.exp(spread * noise) if base else spread * noise
        out[name] = jnp.asarray(drawn.astype(out[name].dtype))
    for name, factor in factors.items():
        out[name] = (out[name] * factor).astype(out[name].dtype)
    return out
```

```python
from contextlib import ExitStack

import concourse.bass as bass
from concourse import mybir

F32 = mybir.dt.float32
I32 = mybir.dt.int32
U32 = mybir.dt.uint32
ALU = mybir.AluOpType
ACT = mybir.ActivationFunctionType

P = 128
F = 26
K = 32
Q4 = P // K
NB = 2048
BLK = 2 * P
BLOCKS = NB // BLK
OCT = 4
H = 128
D1, D2, DC = 512, 256, 16

NA, NX = 13, 5
NY = NA - 2
J0 = NY


def triangle(lo, hi):
    return [(l, l + 1, l, hi) for l in range(lo, hi)]


SEG_A = [(0, NX, NX, NY), (NY, NA, 0, NY), (NY, NY + 1, NY, NA), (NY + 1, NA, NY + 1, NA)]
SEG_XY = triangle(0, NX) + triangle(NX, NY)
SEG_B = triangle(NA, F)


def place(segs, c):
    out = []
    for s in segs:
        out.append((c,) + s)
        c += (s[1] - s[0]) * (s[3] - s[2])
    return out, c


PA, C_XY = place(SEG_A, F)
PXY, C_B = place(SEG_XY, C_XY)
PB, NQ = place(SEG_B, C_B)
R0 = C_B
R1 = NQ - C_XY
N0 = F - J0 + 1
N1 = F + 1
GJ = 9

S_J0, S_U, S_G0, S_J1 = 0, F - J0, F - J0 + 1, F - J0 + 2
S_G1, S_AB = S_J1 + F, S_J1 + F + 1
NS = S_AB + 2
V1W = F * F + 2


def weight_scale(np):
    pair = {}
    for c, l0, l1, m0, m1 in PA + PXY + PB:
        for l in range(l0, l1):
            for m in range(m0, m1):
                pair[c + (l - l0) * (m1 - m0) + m - m0] = (min(l, m), max(l, m))
    w = np.zeros((P, NS), np.float32)
    times = {1: 6, 2: 2, 3: 1}
    for r in range(F, R0):
        l, m = pair[r]
        w[r, S_G0] = 0.5 if l == m else 1.0
        for j in range(max(J0, m), F):
            w[r, S_J0 + j - J0] = 1.0 / times[len({l, m, j})]
    w[:F, S_U] = 1.0
    for r in range(R1):
        l, m = pair[C_XY + r]
        if l >= NA:
            w[r, S_G1] = 0.5 if l == m else 1.0
        for j in range(F):
            own = (j < NA or j >= m) if l >= NA else (j < NY and (j >= m or j < NX <= l))
            if own:
                w[r, S_J1 + j] = 1.0 / times[len({l, m, j})]
    w[:GJ * NA, S_AB] = 1.0
    w[:(F - NA - GJ) * NA, S_AB + 1] = 1.0
    return w


def dlrm_program(nc, ids, tables, dense_t, w1, w2t, b1, b2, wt1, bt1, wt2, bt2, wt3, scale, ident, out):
    with ExitStack() as ctx:
        def sb(name, shape, dt=F32):
            return ctx.enter_context(nc.sbuf_tensor(name + "_sb", shape, dt))

        def sem(name):
            return ctx.enter_context(nc.semaphore(name))

        bank = ctx.enter_context(nc.psum_tensor("bank", [P, 8, 512], F32))
        shared = sb("shared", [P, max(F * V1W, (N0 + N1) * BLK + NS * H)])
        V1 = shared[:, 0:F * V1W].rearrange("p (j x) -> p j x", x=V1W)
        V1p = V1[:, :, 0:F * F].rearrange("p j (l m) -> p j l m", m=F)
        T0 = shared[:, 0:N0 * BLK].rearrange("p (j b) -> p j b", b=BLK)
        T1 = shared[:, N0 * BLK:(N0 + N1) * BLK].rearrange("p (j b) -> p j b", b=BLK)
        V = shared[:, (N0 + N1) * BLK:(N0 + N1) * BLK + NS * H].rearrange("p (s h) -> p s h", h=H)
        Qb = [sb(f"products{u}", [P, max(NQ * K, NS * P)]) for u in range(2)]
        Q = [q[:, 0:NQ * K].rearrange("p (c b) -> p c b", b=K) for q in Qb]
        SP = Qb[1][:, 0:NS * P].rearrange("p (s r) -> p s r", r=P)
        BD = [sb(f"blockdiag{u}", [P, K, Q4, N1]) for u in range(2)]
        E = [sb(f"embedding{u}", [P, F * K]) for u in range(2)]
        idx_all = sb("idx_all", [P, NB // P, F], I32)
        idx = [sb(f"idx{u}", [P, F], I32) for u in range(2)]
        GA = sb("gram_ab", [P, 2, BLK])
        w1_sb = sb("w1", [P, F, F])
        w1s = sb("w1_sym", [P, V1W])
        w2_sb = sb("w2", [P, F, H])
        scale_sb = sb("scale", [P, NS])
        ident_sb = sb("ident", [P, P])
        b_sb = sb("cin_bias", [P, 2])
        bk_sb = sb("cin_bias_k", [P, 2])
        dense_y = sb("dense_and_y", [K + 1, NB])
        dense_sb = dense_y[0:DC, :]
        y_sb = dense_y[K:K + 1, :]
        wt1_sb = sb("w_top1", [P, 2, D1])
        wt1d_sb = sb("w_top1_dense", [DC, D1])
        bt1_sb = sb("b_top1", [P, D1 // P])
        wt2_sb = sb("w_top2", [P, D1 // P, D2])
        bt2_sb = sb("b_top2", [P, D2 // P])
        wt3_sb = sb("w_top3", [P, D2 // P])
        z_sb = sb("z", [P, 2, BLK])
        h1_sb = sb("h1", [P, D1 // P, BLK])
        h2_sb = sb("h2", [P, D2 // P, BLK])

        s_ids = sem("ids_loaded")
        s_wload = sem("cin_weights_loaded")
        s_tload = sem("top_weights_loaded")
        s_zero = sem("zeroed")
        s_w1s = sem("w1_sym_ready")
        s_v1 = sem("v1_products_ready")
        s_v1a = sem("v1_copied_by_act")
        s_v1d = sem("v1_copied_by_dve")
        s_add = sem("weight_sums_step")
        s_vt = sem("weights_transposed")
        s_v = sem("weights_scaled")
        s_bk = sem("cin_bias_ready")
        s_idx = [sem(f"tile_indices_copied{u}") for u in range(2)]
        s_emb = [sem(f"embeddings_gathered{u}") for u in range(2)]
        s_et = [sem(f"embeddings_transposed{u}") for u in range(2)]
        s_q = [sem(f"products_ready{u}") for u in range(2)]
        s_bd = [sem(f"blockdiag_ready{u}") for u in range(2)]
        s_p0 = sem("octet_rows0_ready")
        s_p1 = [sem(f"octet_rows1_ready{u}") for u in range(2)]
        s_e0 = [sem(f"rows0_copied{r}") for r in range(2)]
        s_e1 = [sem(f"rows1_copied{r}") for r in range(2)]
        s_gab = sem("gram_ab_moved")
        s_z = sem("z_ready")
        s_za = sem("z1_copied_by_act")
        s_zd = sem("z2_copied_by_dve")
        s_h1 = sem("h1_ready")
        s_h1a = sem("h1_copied_by_act")
        s_h1d = sem("h1_copied_by_dve")
        s_h2 = sem("h2_ready")
        s_h2a = sem("h2_copied_by_act")
        s_h2d = sem("h2_copied_by_dve")
        s_y = sem("y_ready")
        s_yd = sem("y_copied_by_dve")
        s_out = sem("y_stored")

        FREE = 1
        GATHERED = 16 * F
        W_LOADS = 16 * 7
        T_LOADS = 16 * 7
        QUADS = -(-NS // 4)

        block = ctx.enter_context(nc.Block())

        @block.sync
        def _(sp):
            sp.dma_start(idx_all[:], ids.rearrange("(t p) f -> p t f", p=P)).then_inc(s_ids, 16)
            for dst, src in ((w1_sb[:], w1), (w2_sb[:], w2t), (scale_sb[:], scale), (ident_sb[:], ident),
                             (w1s[:, F * F:F * F + 1], b1), (b_sb[:, 0:1], b1), (b_sb[:, 1:2], b2)):
                sp.dma_start(dst, src).then_inc(s_wload, 16)
            for dst, src in ((dense_sb, dense_t),
                             (wt1_sb[:], wt1[0:2 * H].rearrange("(c p) n -> p c n", p=P)),
                             (wt1d_sb[:], wt1[2 * H:2 * H + DC]),
                             (wt2_sb[:], wt2.rearrange("(c p) n -> p c n", p=P)),
                             (bt1_sb[:], bt1), (bt2_sb[:], bt2), (wt3_sb[:], wt3)):
                sp.dma_start(dst, src).then_inc(s_tload, 16)
            with sp.Fori(0, BLOCKS) as g:
                for r in range(2):
                    sp.wait_ge(s_e0[r], OCT * (g + 1) + FREE)
                sp.wait_ge(s_z, g + FREE)
                for n in range(F - NA):
                    r = n % GJ * NA
                    sp.dma_start(GA[r:r + NA, n // GJ, :], T0[0:NA, NA - J0 + n, :]).then_inc(s_gab, 16)
            sp.wait_ge(s_yd, BLOCKS)
            sp.dma_start(out.rearrange("b o -> o b"), y_sb).then_inc(s_out, 16)
            sp.wait_ge(s_out, 16)

        @block.gpsimd
        def _(pool):
            pool.wait_ge(s_ids, 16)
            with pool.Fori(0, BLOCKS) as g:
                for u in range(2):
                    pool.wait_ge(s_et[u], g + FREE)
                    pool.tensor_copy(idx[u][:], idx_all[:, 2 * g + u, :]).then_inc(s_idx[u], 1)
                    pool.wait_ge(s_idx[u], g + 1)
                    pool.nop(nofuse=True)
                    for f in range(F):
                        pool.indirect_dma_start(
                            out=E[u][:, f * K:(f + 1) * K], out_offset=None, in_=tables[f],
                            in_offset=bass.IndirectOffsetOnAxis(ap=idx[u][:, f:f + 1].bitcast(U32), axis=0),
                        ).then_inc(s_emb[u], 16)

        @block.tensor
        def _(pe):
            pe.wait_ge(s_wload, W_LOADS)
            pe.wait_ge(s_w1s, 1)
            half = V1W // 2
            for j in range(F):
                if j >= 4:
                    pe.wait_ge((s_v1a, s_v1d)[j % 2], (j - 4) // 2 + 1)
                b = j % 4 * 2
                for n in range(2):
                    mm = pe.matmul(bank[:, b + n, 0:half], w2_sb[:, j, :], w1s[:, n * half:(n + 1) * half],
                                   start=True, stop=True)
                mm.then_inc(s_v1, 1)
            pe.wait_ge(s_v1a, F // 2)
            pe.wait_ge(s_v1d, F // 2)
            pe.wait_ge(s_add, 4)
            for i in range(QUADS):
                if i >= 8:
                    pe.wait_ge(s_v, i - 7)
                for s in range(4 * i, min(4 * i + 4, NS)):
                    mm = pe.transpose(bank[:, i % 8, s % 4 * H:(s % 4 + 1) * H], SP[:, s, :], ident_sb[:])
                mm.then_inc(s_vt, 1)
            pe.wait_ge(s_v, QUADS)
            pe.wait_ge(s_tload, T_LOADS)

            pe.sem_inc(s_z, FREE)
            for u in range(2):
                pe.sem_inc(s_p1[u], FREE)
            with pe.Fori(0, BLOCKS) as g:
                for u in range(2):
                    pe.wait_ge(s_q[u], g + 1)
                    pe.wait_ge(s_bd[u], g + 1)
                    for o in range(OCT):
                        r = o % 2
                        pe.wait_ge(s_e0[r], OCT * g + 2 * u + o // 2 + FREE)
                        for b in range(8):
                            mm = pe.matmul(bank[0:R0, r, b * Q4 * N0:(b + 1) * Q4 * N0],
                                           Q[u][:, 0:R0, 8 * o + b], BD[u][:, 8 * o + b, :, J0:N1],
                                           start=True, stop=True)
                        mm.then_inc(s_p0, 1)
                        pe.wait_ge(s_e1[r], OCT * g + 2 * u + o // 2 + FREE)
                        for b in range(8):
                            mm = pe.matmul(bank[0:R1, 2 + 2 * r + b // 4, b % 4 * Q4 * N1:(b % 4 + 1) * Q4 * N1],
                                           Q[u][:, C_XY:NQ, 8 * o + b], BD[u][:, 8 * o + b, :, :],
                                           start=True, stop=True)
                        mm.then_inc(s_p1[u], 1)

                for r in range(2):
                    pe.wait_ge(s_e0[r], OCT * (g + 1) + FREE)
                    pe.wait_ge(s_e1[r], OCT * (g + 1) + FREE)
                for s in range(N0):
                    pe.matmul(bank[:, 6, 0:BLK], V[0:R0, S_J0 + s, :], T0[0:R0, s, :], start=(s == 0), stop=False)
                for s in range(F):
                    pe.matmul(bank[:, 6, 0:BLK], V[0:R1, S_J1 + s, :], T1[0:R1, s, :], start=False, stop=(s == F - 1))
                pe.matmul(bank[:, 7, 0:BLK], V[0:R0, S_G0, :], T0[0:R0, N0 - 1, :], start=True, stop=False)
                pe.matmul(bank[:, 7, 0:BLK], V[0:R1, S_G1, :], T1[0:R1, N1 - 1, :], start=False, stop=False)
                pe.wait_ge(s_gab, 16 * (F - NA) * (g + 1))
                for c, rows in enumerate((GJ * NA, (F - NA - GJ) * NA)):
                    mm = pe.matmul(bank[:, 7, 0:BLK], V[0:rows, S_AB + c, :], GA[0:rows, c, :],
                                   start=False, stop=(c == 1))
                mm.then_inc(s_z, 1)

                pe.wait_ge(s_za, g + 1)
                pe.wait_ge(s_zd, g + 1)
                for c in range(D1 // P):
                    n = slice(c * P, (c + 1) * P)
                    pe.matmul(bank[:, 2 + c, 0:BLK], wt1d_sb[:, n], dense_sb[:, bass.ds(g * BLK, BLK)],
                              start=True, stop=False)
                    pe.matmul(bank[:, 2 + c, 0:BLK], wt1_sb[:, 0, n], z_sb[:, 0, :], start=False, stop=False)
                    pe.matmul(bank[:, 2 + c, 0:BLK], wt1_sb[:, 1, n], z_sb[:, 1, :],
                              start=False, stop=True).then_inc(s_h1, 1)
                pe.wait_ge(s_h1a, 2 * (g + 1))
                pe.wait_ge(s_h1d, 2 * (g + 1))
                for c in range(D2 // P):
                    for k in range(D1 // P):
                        mm = pe.matmul(bank[:, c, 0:BLK], wt2_sb[:, k, c * P:(c + 1) * P], h1_sb[:, k, :],
                                       start=(k == 0), stop=(k == D1 // P - 1))
                    mm.then_inc(s_h2, 1)
                pe.wait_ge(s_h2a, g + 1)
                pe.wait_ge(s_h2d, g + 1)
                for k in range(D2 // P):
                    mm = pe.matmul(bank[0:1, 6, 0:BLK], wt3_sb[:, k:k + 1], h2_sb[:, k, :],
                                   start=(k == 0), stop=(k == D2 // P - 1))
                mm.then_inc(s_y, 1)

        @block.scalar
        def _(act):
            for j in range(0, F, 2):
                act.wait_ge(s_v1, j + 1)
                b = j % 4 * 2
                act.activation(V1[:, j, :].rearrange("p (n x) -> p n x", n=2), bank[:, b:b + 2, 0:V1W // 2],
                               ACT.Copy).then_inc(s_v1a, 1)
            act.wait_ge(s_zero, 1)
            act.wait_ge(s_add, 4)
            T0o = T0.rearrange("p j (u q o b) -> p u o j q b", u=2, q=Q4, o=OCT)
            T1o = T1.rearrange("p j (u q o k b) -> p u o k j q b", u=2, q=Q4, o=OCT, k=2)
            for r in range(2):
                act.sem_inc(s_e0[r], FREE)
                act.sem_inc(s_e1[r], FREE)
            with act.Fori(0, BLOCKS) as g:
                act.wait_ge(s_z, g + FREE)
                for u in range(2):
                    act.wait_ge(s_et[u], g + 1 + FREE)
                    act.wait_ge(s_p1[u], OCT * g + FREE)
                    for q in range(Q4):
                        rows = slice(q * K, (q + 1) * K)
                        ins = act.activation(BD[u][rows, :, q, 0:F],
                                             Q[u][rows, 0:F, :].rearrange("p i b -> p b i"), ACT.Copy)
                    ins.then_inc(s_bd[u], 1)
                    for o in range(OCT):
                        r = o % 2
                        n = 2 * OCT * g + OCT * u + o
                        act.wait_ge(s_p0, n + 1)
                        act.activation(T0o[0:R0, u, o],
                                       bank[0:R0, r, :].rearrange("p (b q j) -> p j q b", b=8, q=Q4),
                                       ACT.Copy).then_inc(s_e0[r], 1)
                        act.wait_ge(s_p1[u], OCT * g + o + 1 + FREE)
                        for k in range(2):
                            ins = act.activation(
                                T1o[0:R1, u, o, k],
                                bank[0:R1, 2 + 2 * r + k, 0:4 * Q4 * N1].rearrange("p (b q j) -> p j q b", b=4, q=Q4),
                                ACT.Copy)
                        ins.then_inc(s_e1[r], 1)
                act.wait_ge(s_bk, 1)
                act.wait_ge(s_z, g + 1 + FREE)
                act.activation(z_sb[:, 0, :], bank[:, 7, 0:BLK], ACT.Identity, bias=bk_sb[:, 0:1]).then_inc(s_za, 1)
                for c in (0, 2):
                    act.wait_ge(s_h1, 4 * g + c + 1)
                    act.activation(h1_sb[:, c, :], bank[:, 2 + c, 0:BLK], ACT.Relu,
                                   bias=bt1_sb[:, c:c + 1]).then_inc(s_h1a, 1)
                act.wait_ge(s_h2, 2 * g + 1)
                act.activation(h2_sb[:, 0, :], bank[:, 0, 0:BLK], ACT.Relu,
                               bias=bt2_sb[:, 0:1]).then_inc(s_h2a, 1)

        @block.vector
        def _(dve):
            for u in range(2):
                dve.sem_inc(s_et[u], FREE)
            dve.memset(w1s[:, F * F + 1:V1W], 0.0)
            dve.wait_ge(s_wload, W_LOADS)
            dve.tensor_tensor(w1s[:, 0:F * F].rearrange("p (l m) -> p l m", m=F), w1_sb[:],
                              w1_sb[:].rearrange("p l m -> p m l"), ALU.add).then_inc(s_w1s, 1)
            dve.tensor_scalar(bk_sb[:], b_sb[:], float(K), None, ALU.mult).then_inc(s_bk, 1)
            for u in range(2):
                dve.memset(BD[u][:], 0.0)
            dve.memset(SP, 0.0).then_inc(s_add, 1)
            dve.wait_ge(s_add, 1)
            for u in range(2):
                for q in range(Q4):
                    ins = dve.memset(BD[u][q * K:(q + 1) * K, :, q, F:N1], 1.0)
            ins.then_inc(s_zero, 1)
            for j in range(1, F, 2):
                dve.wait_ge(s_v1, j + 1)
                b = j % 4 * 2
                dve.tensor_copy(V1[:, j, :].rearrange("p (n x) -> p n x", n=2),
                                bank[:, b:b + 2, 0:V1W // 2]).then_inc(s_v1d, 1)
            dve.wait_ge(s_v1a, F // 2)
            dve.wait_ge(s_v1d, F // 2)

            sums = [(S_J0, J0, F, 0, PA + PXY), (S_J1, 0, NY, C_XY, PXY), (S_J1, 0, F, C_XY, PB)]

            def target(s0, j0, j1, c0, seg):
                c, l0, l1, m0, m1 = seg
                n = (l1 - l0) * (m1 - m0)
                return SP[:, s0:s0 + j1 - j0, c - c0:c - c0 + n].rearrange("p j (l m) -> p j l m", l=l1 - l0)

            for s0, j0, j1, c0, segs in sums:
                for seg in segs:
                    c, l0, l1, m0, m1 = seg
                    ins = dve.tensor_tensor(target(s0, j0, j1, c0, seg), V1p[:, j0:j1, l0:l1, m0:m1],
                                            V1p[:, m0:m1, l0:l1, j0:j1].rearrange("p m l j -> p j l m"), ALU.add)
            ins.then_inc(s_add, 1)
            dve.wait_ge(s_add, 2)
            for s0, j0, j1, c0, segs in sums:
                for seg in segs:
                    c, l0, l1, m0, m1 = seg
                    ins = dve.tensor_tensor(target(s0, j0, j1, c0, seg), target(s0, j0, j1, c0, seg),
                                            V1p[:, l0:l1, m0:m1, j0:j1].rearrange("p l m j -> p j l m"), ALU.add)
            ins.then_inc(s_add, 1)
            w1p = w1s[:, 0:F * F].rearrange("p (l m) -> p l m", m=F)
            dve.tensor_copy(SP[:, S_U, 0:F], V1[:, :, F * F])
            for s, c0, segs in ((S_G0, 0, PA + PXY), (S_G1, C_XY, PB)):
                for c, l0, l1, m0, m1 in segs:
                    n = (l1 - l0) * (m1 - m0)
                    dve.tensor_copy(SP[:, s, c - c0:c - c0 + n].rearrange("p (l m) -> p l m", l=l1 - l0),
                                    w1p[:, l0:l1, m0:m1])
            for c, (ja, jb) in enumerate(((NA, NA + GJ), (NA + GJ, F))):
                ins = dve.tensor_copy(SP[:, S_AB + c, 0:(jb - ja) * NA].rearrange("p (j i) -> p j i", i=NA),
                                      w1p[:, ja:jb, 0:NA])
            ins.then_inc(s_add, 1)
            for i in range(QUADS):
                n = min(4, NS - 4 * i)
                dve.wait_ge(s_vt, i + 1)
                dve.tensor_tensor(V[:, 4 * i:4 * i + n, :],
                                  bank[:, i % 8, 0:n * H].rearrange("p (s h) -> p s h", h=H),
                                  scale_sb[:, 4 * i:4 * i + n].unsqueeze(2).broadcast_to([P, n, H]),
                                  ALU.mult).then_inc(s_v, 1)

            with dve.Fori(0, BLOCKS) as g:
                for u in range(2):
                    dve.wait_ge(s_emb[u], GATHERED * (g + 1))
                    dve.wait_ge(s_p1[u], OCT * g + FREE)
                    dve.transpose(Q[u][:, 0:F, :].rearrange("p i b -> p (i b)"), E[u][:]).then_inc(s_et[u], 1)
                    dve.wait_ge(s_et[u], g + 1 + FREE)
                    for c, l0, l1, m0, m1 in PA + PXY + PB:
                        L, M = l1 - l0, m1 - m0
                        ins = dve.tensor_tensor(
                            Q[u][:, c:c + L * M, :].rearrange("p (l m) b -> p l m b", l=L),
                            Q[u][:, l0:l1, :].unsqueeze(2).broadcast_to([P, L, M, K]),
                            Q[u][:, m0:m1, :].unsqueeze(1).broadcast_to([P, L, M, K]), ALU.mult)
                    ins.then_inc(s_q[u], 1)
                dve.wait_ge(s_z, g + 1 + FREE)
                dve.tensor_scalar(z_sb[:, 1, :], bank[:, 6, 0:BLK], bk_sb[:, 1:2], None, ALU.add).then_inc(s_zd, 1)
                for c in (1, 3):
                    dve.wait_ge(s_h1, 4 * g + c + 1)
                    dve.tensor_scalar(h1_sb[:, c, :], bank[:, 2 + c, 0:BLK], bt1_sb[:, c:c + 1], 0.0,
                                      ALU.add, ALU.max).then_inc(s_h1d, 1)
                dve.wait_ge(s_h2, 2 * g + 2)
                dve.tensor_scalar(h2_sb[:, 1, :], bank[:, 1, 0:BLK], bt2_sb[:, 1:2], 0.0,
                                  ALU.add, ALU.max).then_inc(s_h2d, 1)
                dve.wait_ge(s_y, g + 1)
                dve.tensor_copy(y_sb[:, bass.ds(g * BLK, BLK)], bank[0:1, 6, 0:BLK]).then_inc(s_yd, 1)


def kernel(**inputs):
    import numpy as np
    import concourse.bacc as bacc
    from concourse import mybir
    from concourse.bass_utils import run_bass_kernel_spmd as run

    nc = bacc.Bacc("TRN2", target_bir_lowering=False, num_devices=1)
    arrays = {}

    def given(name, a):
        arrays[name] = np.ascontiguousarray(a)
        return nc.dram_tensor(name, arrays[name].shape, mybir.dt.from_np(arrays[name].dtype),
                              kind="ExternalInput").ap()

    args = [
        given("ids", inputs["ids"]),
        [given(f"tbl_{f}", inputs[f"tbl_{f}"]) for f in range(F)],
        given("dense_t", np.asarray(inputs["dense_ctx"]).T),
        given("w1", inputs["L0_rec_W1"]),
        given("w2t", np.asarray(inputs["L0_rec_W2"]).transpose(1, 2, 0)),
        given("b1", np.asarray(inputs["L0_rec_b1"]).reshape(H, 1)),
        given("b2", np.asarray(inputs["L0_rec_b2"]).reshape(H, 1)),
        given("w_top1_in", inputs["W_top1"]),
        given("b_top1_in", np.asarray(inputs["b_top1"]).reshape(D1 // P, P).T),
        given("w_top2_in", inputs["W_top2"]),
        given("b_top2_in", np.asarray(inputs["b_top2"]).reshape(D2 // P, P).T),
        given("w_top3_in", np.asarray(inputs["W_top3"]).reshape(D2 // P, P).T),
        given("weight_scale", weight_scale(np)),
        given("identity", np.eye(P, dtype=np.float32)),
    ]
    out = nc.dram_tensor("y_out", (NB, 1), F32, kind="ExternalOutput").ap()
    dlrm_program(nc, *args, out)
    return run(nc, [arrays], core_ids=[0]).results[0]["y_out"]
```

```python
from contextlib import ExitStack

import concourse.bass as bass
from concourse import mybir

F32 = mybir.dt.float32
I32 = mybir.dt.int32
U32 = mybir.dt.uint32
ALU = mybir.AluOpType
ACT = mybir.ActivationFunctionType

P = 128
F = 26
K = 32
Q4 = P // K
NB = 2048
BLK = 2 * P
BLOCKS = NB // BLK
OCT = 4
H = 128
D1, D2, DC = 512, 256, 16

P1, P2, C2, C1, S1, S2 = 0, 4, 8, 13, 15, 20
NA = C1


def triangle(lo, hi):
    return [(l, l + 1, l, hi) for l in range(lo, hi)]


def place(segs, c):
    out = []
    for s in segs:
        out.append((c,) + s)
        c += (s[1] - s[0]) * (s[3] - s[2])
    return out, c


SEG_A, C_S = place(triangle(C1, S1) + [(C1, S1, S1, F), (S1, S2, S2, F)], F)
SEG_S, C_ONE = place(triangle(S1, S2) + triangle(S2, F), C_S)
SEG_P, C_B = place(triangle(P1, P2) + triangle(P2, C2), C_ONE + 1)
SEG_B, NQ = place([(P1, P2, P2, C2), (P1, C2, C2, C1)] + triangle(C2, C1), C_B)
LO0, HI0 = NA, C_B
LO1, HI1 = C_S, NQ
R0, R1 = HI0 - LO0, HI1 - LO1
N0 = 1 + S1
N1 = F - C2 + 1
NC = F + 2
GJ = 9

S_G0 = 0
S_J0 = 1
S_J1 = S_J0 + S1
S_G1 = S_J1 + F - C2
S_AB = S_G1 + 1
NS = S_AB + 2
V1W = NA * F + (F - NA) ** 2 + 1
assert R0 <= P and R1 <= P and N0 * Q4 * 8 <= 512 and N1 * Q4 * 4 <= 512 and V1W <= 512


def weight_scale(np):
    pair = {}
    for c, l0, l1, m0, m1 in SEG_A + SEG_S + SEG_P + SEG_B:
        for l in range(l0, l1):
            for m in range(m0, m1):
                pair[c + (l - l0) * (m1 - m0) + m - m0] = (l, m)
    w = np.zeros((P, NS), np.float32)
    times = {1: 6, 2: 2, 3: 1}
    for c, (l, m) in pair.items():
        once = {j: 1.0 / times[len({l, m, j})] for j in range(F)}
        if LO0 <= c < HI0:
            r = c - LO0
            if l >= NA:
                w[r, S_G0] = 0.5 if l == m else 1.0
                js = [j for j in range(S1) if j < NA or j <= l]
            else:
                js = [j for j in range(C2) if j >= m or (j < P2 <= l)]
            for j in js:
                w[r, S_J0 + j] = once[j]
        if LO1 <= c < HI1:
            r = c - LO1
            if l < NA:
                w[r, S_G1] = 0.5 if l == m else 1.0
                js = [j for j in range(C2, F) if j >= m]
            else:
                js = [j for j in range(S1, F) if j >= m or (j < S2 <= l)]
            for j in js:
                w[r, S_J1 + j - C2] = once[j]
    w[C_ONE - LO0, S_J0:S_J0 + S1] = 1.0
    w[C_ONE - LO1, S_J1 + S1 - C2:S_J1 + F - C2] = 1.0
    w[:GJ * NA, S_AB] = 1.0
    w[:(NA - GJ) * NA, S_AB + 1] = 1.0
    return w


def dlrm_program(nc, ids, tables, dense_t, w1, w2t, b1, b2, wt1, bt1, wt2, bt2, wt3, scale, ident, out):
    with ExitStack() as ctx:
        def sb(name, shape, dt=F32):
            return ctx.enter_context(nc.sbuf_tensor(name + "_sb", shape, dt))

        def sem(name):
            return ctx.enter_context(nc.semaphore(name))

        bank = ctx.enter_context(nc.psum_tensor("bank", [P, 8, 512], F32))
        T_BANK = (0, 1)
        HALF_BANK = (2, 3)
        Z_BANK = (7, 6)
        T_W, V_W = (N0 + N1) * BLK, NS * H
        shared = sb("shared", [P, max(F * V1W, T_W + V_W)])
        V1 = shared[:, 0:F * V1W].rearrange("p (j x) -> p j x", x=V1W)
        T0 = shared[:, 0:N0 * BLK].rearrange("p (j b) -> p j b", b=BLK)
        T1 = shared[:, N0 * BLK:T_W].rearrange("p (j b) -> p j b", b=BLK)
        V = shared[:, T_W:T_W + V_W].rearrange("p (s h) -> p s h", h=H)
        Q = [sb(f"products{u}", [P, NQ, K]) for u in range(2)]
        SP = Q[1][:].rearrange("p c b -> p (c b)")[:, 0:NS * P].rearrange("p (s r) -> p s r", r=P)
        BD = [sb(f"blockdiag{u}", [P, K, Q4, NC]) for u in range(2)]
        E = [sb(f"embedding{u}", [P, F * K]) for u in range(2)]
        idx_all = sb("idx_all", [P, NB // P, F], I32)
        idx = [sb(f"idx{u}", [P, F], I32) for u in range(2)]
        GA = sb("gram_ab", [P, 2, BLK])
        w1_sb = sb("w1", [P, F, F])
        w1s = sb("w1_sym", [P, V1W])
        w2_sb = sb("w2", [P, F, H])
        scale_sb = sb("scale", [P, NS])
        ident_sb = sb("ident", [P, P])
        b_sb = sb("cin_bias", [P, 2])
        bk_sb = sb("cin_bias_k", [P, 2])
        dense_sb = sb("dense", [DC, NB])
        wt1_sb = sb("w_top1", [P, 2, D1])
        wt1d_sb = sb("w_top1_dense", [DC, D1])
        bt1_sb = sb("b_top1", [P, D1 // P])
        wt2_sb = sb("w_top2", [P, D1 // P, D2])
        bt2_sb = sb("b_top2", [P, D2 // P])
        wt3_sb = sb("w_top3", [P, D2 // P])
        z_sb = sb("z", [P, 2, BLK])
        h1_sb = sb("h1", [P, D1 // P, BLK])
        h2_sb = sb("h2", [P, D2 // P, BLK])
        y_sb = sb("y", [1, BLK])

        s_ids = sem("ids_loaded")
        s_w1load = sem("w1_loaded")
        s_w2load = [sem(f"w2_loaded{n}") for n in range(2)]
        s_cload = sem("constants_loaded")
        s_tload = sem("top_weights_loaded")
        s_zero = sem("blockdiag_zeroed")
        s_ones = sem("blockdiag_ones")
        s_w1s = sem("w1_sym_ready")
        s_v1 = sem("v1_products_ready")
        s_v1c = [sem("v1_copied_by_act"), sem("v1_copied_by_dve")]
        s_add = sem("weight_sums_step")
        s_vt = sem("weights_transposed")
        s_v = sem("weights_scaled")
        s_bk = sem("cin_bias_ready")
        s_idx = [sem(f"tile_indices_copied{u}") for u in range(2)]
        s_emb = [sem(f"embeddings_gathered{u}") for u in range(2)]
        s_et = [sem(f"embeddings_transposed{u}") for u in range(2)]
        s_q = [sem(f"tile_operands_ready{u}") for u in range(2)]
        s_p0 = sem("octet_rows0_ready")
        s_p1 = [sem(f"half_rows1_ready{u}") for u in range(2)]
        s_e0 = [sem(f"rows0_copied{r}") for r in range(2)]
        s_e1 = [sem(f"rows1_copied{k}") for k in range(2)]
        s_gab = sem("gram_ab_moved")
        s_z2 = sem("z2_ready")
        s_z1 = sem("z1_ready")
        s_zc = sem("z_copied")
        s_h1 = sem("h1_ready")
        s_h1c = sem("h1_copied")
        s_h2 = sem("h2_ready")
        s_h2c = sem("h2_copied")
        s_y = sem("y_ready")
        s_yc = sem("y_copied")
        s_out = sem("y_stored")

        FREE = 1
        GATHERED = 16 * F
        HALVES = 2 * OCT
        QUADS = -(-NS // 4)
        M1, M2 = D1 // P, D2 // P

        block = ctx.enter_context(nc.Block())

        @block.sync
        def _(sp):
            sp.dma_start(w1_sb[:], w1).then_inc(s_w1load, 16)
            sp.dma_start(w1s[:, V1W - 1:V1W], b1).then_inc(s_w1load, 16)
            sp.dma_start(w2_sb[:, 0:6, :], w2t[:, 0:6, :]).then_inc(s_w2load[0], 16)
            sp.dma_start(w2_sb[:, 6:F, :], w2t[:, 6:F, :]).then_inc(s_w2load[1], 16)
            for dst, src in ((scale_sb[:], scale), (ident_sb[:], ident), (b_sb[:, 0:1], b1), (b_sb[:, 1:2], b2)):
                sp.dma_start(dst, src).then_inc(s_cload, 16)
            for dst, src in ((dense_sb[:], dense_t),
                             (wt1_sb[:], wt1[0:2 * H].rearrange("(c p) n -> p c n", p=P)),
                             (wt1d_sb[:], wt1[2 * H:2 * H + DC]),
                             (wt2_sb[:], wt2.rearrange("(c p) n -> p c n", p=P)),
                             (bt1_sb[:], bt1), (bt2_sb[:], bt2), (wt3_sb[:], wt3)):
                sp.dma_start(dst, src).then_inc(s_tload, 16)

            def spread_gram(g):
                for r in range(2):
                    sp.wait_ge(s_e0[r], OCT * (g + 1) + FREE)
                for j in range(NA):
                    r = j % GJ * NA
                    sp.dma_start(GA[r:r + NA, j // GJ, :], T0[0:NA, 1 + j, :]).then_inc(s_gab, 16)

            def store(g):
                sp.wait_ge(s_yc, g + 1)
                sp.dma_start(out.rearrange("(g b) o -> g o b", b=BLK)[g], y_sb[:]).then_inc(s_out, 16)

            spread_gram(0)
            with sp.Fori(1, BLOCKS) as g:
                spread_gram(g)
                store(g - 1)
            store(BLOCKS - 1)
            sp.wait_ge(s_out, 16 * (BLOCKS + FREE))

        @block.gpsimd
        def _(pool):
            pool.wait_ge(s_ids, 16)
            with pool.Fori(0, BLOCKS) as g:
                for u in range(2):
                    pool.wait_ge(s_et[u], g + FREE)
                    pool.tensor_copy(idx[u][:], idx_all[:, 2 * g + u, :]).then_inc(s_idx[u], 1)
                    pool.wait_ge(s_idx[u], g + 1)
                    pool.nop(nofuse=True)
                    for f in range(F):
                        pool.indirect_dma_start(
                            out=E[u][:, f * K:(f + 1) * K], out_offset=None, in_=tables[f],
                            in_offset=bass.IndirectOffsetOnAxis(ap=idx[u][:, f:f + 1].bitcast(U32), axis=0),
                        ).then_inc(s_emb[u], 16)

        @block.tensor
        def _(pe):
            pe.wait_ge(s_w1load, 32)
            pe.wait_ge(s_w1s, 1)
            for j in range(F):
                if j in (0, 6):
                    pe.wait_ge(s_w2load[j // 6], 16)
                if j >= 8:
                    pe.wait_ge(s_v1c[j % 2], (j - 8) // 2 + 1)
                pe.matmul(bank[:, j % 8, 0:V1W], w2_sb[:, j, :], w1s[:], start=True, stop=True).then_inc(s_v1, 1)
            for k in range(2):
                pe.wait_ge(s_v1c[k], F // 2)
            pe.wait_ge(s_add, 4)
            pe.wait_ge(s_cload, 16 * 4)
            for i in range(QUADS):
                if i >= 8:
                    pe.wait_ge(s_v, i - 7)
                for s in range(4 * i, min(4 * i + 4, NS)):
                    mm = pe.transpose(bank[:, i % 8, s % 4 * H:(s % 4 + 1) * H], SP[:, s, :], ident_sb[:])
                mm.then_inc(s_vt, 1)
            pe.wait_ge(s_v, QUADS)
            pe.sem_inc(s_z1, FREE)
            for u in range(2):
                pe.sem_inc(s_p1[u], FREE)

            def tile_sums(g, u):
                pe.wait_ge(s_q[u], g + 1)
                for o in range(OCT):
                    r = o % 2
                    pe.wait_ge(s_e0[r], OCT * g + 2 * u + o // 2 + FREE)
                    for b in range(8):
                        mm = pe.matmul(bank[0:R0, T_BANK[r], b * Q4 * N0:(b + 1) * Q4 * N0],
                                       Q[u][:, LO0:HI0, 8 * o + b], BD[u][:, 8 * o + b, :, 0:N0],
                                       start=True, stop=True)
                    mm.then_inc(s_p0, 1)
                    for k in range(2):
                        pe.wait_ge(s_e1[k], HALVES * g + OCT * u + o + FREE)
                        for b in range(4):
                            mm = pe.matmul(bank[0:R1, HALF_BANK[k], b * Q4 * N1:(b + 1) * Q4 * N1],
                                           Q[u][:, LO1:HI1, 8 * o + 4 * k + b],
                                           BD[u][:, 8 * o + 4 * k + b, :, NC - N1:NC], start=True, stop=True)
                        mm.then_inc(s_p1[u], 1)

            def z_rows0(g):
                for r in range(2):
                    pe.wait_ge(s_e0[r], OCT * (g + 1) + FREE)
                for s in range(1, N0):
                    pe.matmul(bank[:, Z_BANK[1], 0:BLK], V[0:R0, s, :], T0[0:R0, s, :], start=(s == 1), stop=False)

            def z_rest(g):
                for k in range(2):
                    pe.wait_ge(s_e1[k], HALVES * (g + 1) + FREE)
                for s in range(N1 - 1):
                    mm = pe.matmul(bank[:, Z_BANK[1], 0:BLK], V[0:R1, S_J1 + s, :], T1[0:R1, s, :],
                                   start=False, stop=(s == N1 - 2))
                mm.then_inc(s_z2, 1)
                pe.matmul(bank[:, Z_BANK[0], 0:BLK], V[0:R0, S_G0, :], T0[0:R0, 0, :], start=True, stop=False)
                pe.matmul(bank[:, Z_BANK[0], 0:BLK], V[0:R1, S_G1, :], T1[0:R1, N1 - 1, :], start=False, stop=False)
                pe.wait_ge(s_gab, 16 * NA * (g + 1))
                for c, rows in enumerate((GJ * NA, (NA - GJ) * NA)):
                    mm = pe.matmul(bank[:, Z_BANK[0], 0:BLK], V[0:rows, S_AB + c, :], GA[0:rows, c, :],
                                   start=False, stop=(c == 1))
                mm.then_inc(s_z1, 1)

            def top1(g):
                pe.wait_ge(s_zc, 2 * (g + 1))
                for c in range(M1):
                    n = slice(c * P, (c + 1) * P)
                    h = bank[:, Z_BANK[c % 2], 0:BLK]
                    if c >= 2:
                        pe.wait_ge(s_h1c, M1 * g + c - 1)
                    pe.matmul(h, wt1_sb[:, 0, n], z_sb[:, 0, :], start=True, stop=False)
                    pe.matmul(h, wt1_sb[:, 1, n], z_sb[:, 1, :], start=False, stop=False)
                    pe.matmul(h, wt1d_sb[:, n], dense_sb[:, bass.ds(g * BLK, BLK)],
                              start=False, stop=True).then_inc(s_h1, 1)

            def top2(g):
                pe.wait_ge(s_h1c, M1 * (g + 1))
                for c in range(M2):
                    for k in range(M1):
                        mm = pe.matmul(bank[:, Z_BANK[1 - c], 0:BLK], wt2_sb[:, k, c * P:(c + 1) * P], h1_sb[:, k, :],
                                       start=(k == 0), stop=(k == M1 - 1))
                    mm.then_inc(s_h2, 1)

            def top3(g):
                pe.wait_ge(s_h2c, M2 * (g + 1))
                for k in range(M2):
                    mm = pe.matmul(bank[0:1, Z_BANK[0], 0:BLK], wt3_sb[:, k:k + 1], h2_sb[:, k, :],
                                   start=(k == 0), stop=(k == M2 - 1))
                mm.then_inc(s_y, 1)

            tile_sums(0, 0)
            tile_sums(0, 1)
            z_rows0(0)
            z_rest(0)
            pe.wait_ge(s_tload, 16 * 7)
            with pe.Fori(1, BLOCKS) as g:
                tile_sums(g, 0)
                top1(g - 1)
                tile_sums(g, 1)
                top2(g - 1)
                pe.wait_ge(s_h2c, M2 * (g - 1) + 1)
                z_rows0(g)
                top3(g - 1)
                pe.wait_ge(s_yc, g)
                z_rest(g)
            top1(BLOCKS - 1)
            top2(BLOCKS - 1)
            top3(BLOCKS - 1)

        @block.scalar
        def _(act):
            act.dma_start(idx_all[:], ids.rearrange("(t p) f -> p t f", p=P)).then_inc(s_ids, 16)
            for u in range(2):
                ins = act.memzero(BD[u][:])
            ins.then_inc(s_zero, 1)
            for j in range(0, F, 2):
                act.wait_ge(s_v1, j + 1)
                act.activation(V1[:, j, :], bank[:, j % 8, 0:V1W], ACT.Copy).then_inc(s_v1c[0], 1)
            act.wait_ge(s_add, 4)
            act.wait_ge(s_cload, 16 * 4)
            act.wait_ge(s_tload, 16 * 7)
            act.mul(bk_sb[:], b_sb[:], float(K)).then_inc(s_bk, 1)
            act.wait_ge(s_bk, 1)
            act.sem_inc(s_out, 16 * FREE)
            for r in range(2):
                act.sem_inc(s_e0[r], FREE)
                act.sem_inc(s_e1[r], FREE)
            T0o = T0.rearrange("p j (u q o b) -> p u o j q b", u=2, q=Q4, o=OCT)
            T1o = T1.rearrange("p j (u q o k b) -> p u o k j q b", u=2, q=Q4, o=OCT, k=2)

            def copy_sums(g, u):
                if u == 0:
                    act.wait_ge(s_z1, g + FREE)
                for o in range(OCT):
                    r = o % 2
                    act.wait_ge(s_p0, HALVES * g + OCT * u + o + 1)
                    act.activation(T0o[0:R0, u, o],
                                   bank[0:R0, T_BANK[r], :].rearrange("p (b q j) -> p j q b", b=8, q=Q4),
                                   ACT.Copy).then_inc(s_e0[r], 1)
                    for k in range(2):
                        act.wait_ge(s_p1[u], HALVES * g + 2 * o + k + 1 + FREE)
                        act.activation(T1o[0:R1, u, o, k],
                                       bank[0:R1, HALF_BANK[k], 0:4 * Q4 * N1].rearrange(
                                           "p (b q j) -> p j q b", b=4, q=Q4),
                                       ACT.Copy).then_inc(s_e1[k], 1)

            def copy_z(g):
                act.wait_ge(s_z2, g + 1)
                act.activation(z_sb[:, 1, :], bank[:, Z_BANK[1], 0:BLK], ACT.Identity,
                               bias=bk_sb[:, 1:2]).then_inc(s_zc, 1)
                act.wait_ge(s_z1, g + 1 + FREE)
                act.activation(z_sb[:, 0, :], bank[:, Z_BANK[0], 0:BLK], ACT.Identity,
                               bias=bk_sb[:, 0:1]).then_inc(s_zc, 1)

            def copy_h1(g):
                for c in range(M1):
                    act.wait_ge(s_h1, M1 * g + c + 1)
                    act.activation(h1_sb[:, c, :], bank[:, Z_BANK[c % 2], 0:BLK], ACT.Relu,
                                   bias=bt1_sb[:, c:c + 1]).then_inc(s_h1c, 1)

            def copy_h2(g):
                for c in range(M2):
                    act.wait_ge(s_h2, M2 * g + c + 1)
                    act.activation(h2_sb[:, c, :], bank[:, Z_BANK[1 - c], 0:BLK], ACT.Relu,
                                   bias=bt2_sb[:, c:c + 1]).then_inc(s_h2c, 1)

            def copy_y(g):
                act.wait_ge(s_out, 16 * (g + FREE))
                act.wait_ge(s_y, g + 1)
                act.activation(y_sb[:], bank[0:1, Z_BANK[0], 0:BLK], ACT.Copy).then_inc(s_yc, 1)

            copy_sums(0, 0)
            copy_sums(0, 1)
            copy_z(0)
            with act.Fori(1, BLOCKS) as g:
                copy_sums(g, 0)
                copy_h1(g - 1)
                copy_sums(g, 1)
                copy_h2(g - 1)
                copy_y(g - 1)
                copy_z(g)
            copy_h1(BLOCKS - 1)
            copy_h2(BLOCKS - 1)
            copy_y(BLOCKS - 1)

        @block.vector
        def _(dve):
            for u in range(2):
                dve.sem_inc(s_et[u], FREE)

            def pairs(t, j0, j1, l0, l1, m0, m1):
                low = t[:, :, 0:NA * F].rearrange("p j (l m) -> p j l m", m=F)
                high = t[:, :, NA * F:V1W - 1].rearrange("p j (l m) -> p j l m", m=F - NA)
                if l1 <= NA:
                    return low[:, j0:j1, l0:l1, m0:m1]
                if m1 <= NA:
                    return low[:, j0:j1, m0:m1, l0:l1].rearrange("p j m l -> p j l m")
                return high[:, j0:j1, l0 - NA:l1 - NA, m0 - NA:m1 - NA]

            w1v = w1s[:].unsqueeze(1)
            turned = w1_sb[:].rearrange("p m l -> p l m")
            dve.wait_ge(s_w1load, 32)
            dve.tensor_tensor(pairs(w1v, 0, 1, 0, NA, 0, F).squeeze(1), w1_sb[:, 0:NA, :], turned[:, 0:NA, :], ALU.add)
            dve.tensor_tensor(pairs(w1v, 0, 1, NA, F, NA, F).squeeze(1), w1_sb[:, NA:F, NA:F],
                              turned[:, NA:F, NA:F], ALU.add).then_inc(s_w1s, 1)
            dve.memset(SP, 0.0).then_inc(s_add, 1)
            dve.memset(Q[0][:, C_ONE, :], 1.0)
            dve.wait_ge(s_zero, 1)
            for u in range(2):
                for q in range(Q4):
                    for c in (0, NC - 1):
                        ins = dve.memset(BD[u][q * K:(q + 1) * K, :, q, c:c + 1], 1.0)
            ins.then_inc(s_ones, 1)
            for j in range(1, F, 2):
                dve.wait_ge(s_v1, j + 1)
                dve.tensor_copy(V1[:, j, :], bank[:, j % 8, 0:V1W]).then_inc(s_v1c[1], 1)
            for k in range(2):
                dve.wait_ge(s_v1c[k], F // 2)
            dve.wait_ge(s_add, 1)
            dve.wait_ge(s_w1s, 1)

            sums = [(S_J0, LO0, 0, NA, SEG_A + SEG_S), (S_J0, LO0, NA, S1, SEG_A + SEG_S), (S_J0, LO0, 0, C2, SEG_P),
                    (S_J1 - C2, LO1, S1, F, SEG_S), (S_J1 - C2, LO1, C2, F, SEG_P + SEG_B)]
            parts = [(s0, c0, j0, j1, seg) for s0, c0, j0, j1, segs in sums for seg in segs]

            def target(s0, c0, j0, j1, seg):
                c, l0, l1, m0, m1 = seg
                n = (l1 - l0) * (m1 - m0)
                return SP[:, s0 + j0:s0 + j1, c - c0:c - c0 + n].rearrange("p j (l m) -> p j l m", l=l1 - l0)

            for s0, c0, j0, j1, seg in parts:
                _, l0, l1, m0, m1 = seg
                ins = dve.tensor_tensor(target(s0, c0, j0, j1, seg), pairs(V1, j0, j1, l0, l1, m0, m1),
                                        pairs(V1, m0, m1, l0, l1, j0, j1).rearrange("p m l j -> p j l m"), ALU.add)
            ins.then_inc(s_add, 1)
            dve.wait_ge(s_add, 2)
            for s0, c0, j0, j1, seg in parts:
                _, l0, l1, m0, m1 = seg
                ins = dve.tensor_tensor(target(s0, c0, j0, j1, seg), target(s0, c0, j0, j1, seg),
                                        pairs(V1, l0, l1, m0, m1, j0, j1).rearrange("p l m j -> p j l m"), ALU.add)
            ins.then_inc(s_add, 1)
            dve.tensor_copy(SP[:, S_J0:S_J0 + S1, C_ONE - LO0], V1[:, 0:S1, V1W - 1])
            dve.tensor_copy(SP[:, S_J1 + S1 - C2:S_J1 + F - C2, C_ONE - LO1], V1[:, S1:F, V1W - 1])
            for s, c0, segs in ((S_G0, LO0, SEG_A + SEG_S), (S_G1, LO1, SEG_P + SEG_B)):
                for c, l0, l1, m0, m1 in segs:
                    n = (l1 - l0) * (m1 - m0)
                    dve.tensor_copy(SP[:, s:s + 1, c - c0:c - c0 + n].rearrange("p s (l m) -> p s l m", l=l1 - l0),
                                    pairs(w1v, 0, 1, l0, l1, m0, m1))
            for c, (ja, jb) in enumerate(((0, GJ), (GJ, NA))):
                ins = dve.tensor_copy(
                    SP[:, S_AB + c:S_AB + c + 1, 0:(jb - ja) * (F - NA)].rearrange("p s (j i) -> p s j i", i=F - NA),
                    pairs(w1v, 0, 1, ja, jb, NA, F))
            ins.then_inc(s_add, 1)
            dve.wait_ge(s_cload, 16 * 4)
            for i in range(QUADS):
                n = min(4, NS - 4 * i)
                dve.wait_ge(s_vt, i + 1)
                dve.tensor_tensor(V[:, 4 * i:4 * i + n, :],
                                  bank[:, i % 8, 0:n * H].rearrange("p (s h) -> p s h", h=H),
                                  scale_sb[:, 4 * i:4 * i + n].unsqueeze(2).broadcast_to([P, n, H]),
                                  ALU.mult).then_inc(s_v, 1)
            dve.memset(Q[1][:, C_ONE, :], 1.0)

            with dve.Fori(0, BLOCKS) as g:
                for u in range(2):
                    dve.wait_ge(s_emb[u], GATHERED * (g + 1))
                    dve.wait_ge(s_p1[u], HALVES * g + FREE)
                    dve.transpose(Q[u][:, 0:F, :].rearrange("p i b -> p (i b)"), E[u][:]).then_inc(s_et[u], 1)
                    dve.wait_ge(s_et[u], g + 1 + FREE)
                    for q in range(Q4):
                        rows = slice(q * K, (q + 1) * K)
                        dve.tensor_copy(BD[u][rows, :, q, 1:1 + F], Q[u][rows, 0:F, :].rearrange("p i b -> p b i"))
                    for c, l0, l1, m0, m1 in SEG_A + SEG_S + SEG_P + SEG_B:
                        L, M = l1 - l0, m1 - m0
                        ins = dve.tensor_tensor(
                            Q[u][:, c:c + L * M, :].rearrange("p (l m) b -> p l m b", l=L),
                            Q[u][:, l0:l1, :].unsqueeze(2).broadcast_to([P, L, M, K]),
                            Q[u][:, m0:m1, :].unsqueeze(1).broadcast_to([P, L, M, K]), ALU.mult)
                    ins.then_inc(s_q[u], 1)


def kernel(**inputs):
    import numpy as np
    import concourse.bacc as bacc
    from concourse import mybir
    from concourse.bass_utils import run_bass_kernel_spmd as run

    nc = bacc.Bacc("TRN2", target_bir_lowering=False, num_devices=1)
    arrays = {}

    def given(name, a):
        arrays[name] = np.ascontiguousarray(a)
        return nc.dram_tensor(name, arrays[name].shape, mybir.dt.from_np(arrays[name].dtype),
                              kind="ExternalInput").ap()

    args = [
        given("ids", inputs["ids"]),
        [given(f"tbl_{f}", inputs[f"tbl_{f}"]) for f in range(F)],
        given("dense_t", np.asarray(inputs["dense_ctx"]).T),
        given("w1", inputs["L0_rec_W1"]),
        given("w2t", np.asarray(inputs["L0_rec_W2"]).transpose(1, 2, 0)),
        given("b1", np.asarray(inputs["L0_rec_b1"]).reshape(H, 1)),
        given("b2", np.asarray(inputs["L0_rec_b2"]).reshape(H, 1)),
        given("w_top1_in", inputs["W_top1"]),
        given("b_top1_in", np.asarray(inputs["b_top1"]).reshape(D1 // P, P).T),
        given("w_top2_in", inputs["W_top2"]),
        given("b_top2_in", np.asarray(inputs["b_top2"]).reshape(D2 // P, P).T),
        given("w_top3_in", np.asarray(inputs["W_top3"]).reshape(D2 // P, P).T),
        given("weight_scale", weight_scale(np)),
        given("identity", np.eye(P, dtype=np.float32)),
    ]
    out = nc.dram_tensor("y_out", (NB, 1), F32, kind="ExternalOutput").ap()
    dlrm_program(nc, *args, out)
    return run(nc, [arrays], core_ids=[0]).results[0]["y_out"]
```

```python
from contextlib import ExitStack

import concourse.bass as bass
from concourse import mybir

F32 = mybir.dt.float32
BF16 = mybir.dt.bfloat16
I32 = mybir.dt.int32
U32 = mybir.dt.uint32
ALU = mybir.AluOpType
ACT = mybir.ActivationFunctionType

P = 128
F = 26
K = 32
Q4 = P // K
NB = 2048
BLK = 2 * P
BLOCKS = NB // BLK
TILES = NB // P
OCT = 4
H = 128
D1, D2, DC = 512, 256, 16

C, X, Y = 0, 10, 18
GROUPS = ((C, X), (X, Y), (Y, F))
ARRIVAL = ((X, Y), (Y, F), (C, X))


def place(segs, c):
    out = []
    for s in segs:
        out.append((c,) + s)
        c += (s[1] - s[0]) * (s[3] - s[2])
    return out, c


SEG_XY, XYR = place([(X, Y, Y, F)], 0)
NF = F - X
C_ONE = XYR + F
SEG_IN, NQ = place([(l, l + 1, l, hi) for lo, hi in GROUPS for l in range(lo, hi)], C_ONE + 1)
LO1, HI1 = C_ONE, NQ
R0, R1 = XYR + NF, HI1 - LO1
N0 = 1 + X
N1 = 1 + F


def field_columns(lo, hi):
    c = XYR + (NF if lo < X else -X)
    return slice(c + lo, c + hi)


XH = X // 2
NG = (P - XYR) // NF
S_XY, S_XYC = 0, 1
S_G = S_XYC + XH
S_1 = S_G + 1
NS = S_1 + N1
assert 2 * XYR == P and (X - NG) * NF <= P
V1_C = 0
V1_X = V1_C + X * F
V1_Y = V1_X + (Y - X) * (F - X)
V1_U = V1_Y + (F - Y) ** 2
V1W = V1_U + 1
DPARTS = "hhmmlh"
WPARTS = "hmhmhl"

LOOKUP, LR = {1: 1000, 5: 1000, 9: 1250}, 125
CHUNK0 = {}
LCH = 0
for _f, _rows in LOOKUP.items():
    CHUNK0[_f] = LCH
    LCH += _rows // LR
NL, PARTS = len(LOOKUP), 3
assert all(C <= f < X for f in LOOKUP) and NL * PARTS * K <= 512 and NL >= PARTS - 1
assert R0 <= P and R1 <= P and N0 * Q4 * 8 <= 512 and N1 * Q4 * 4 <= 512 and V1W <= 512
DG = P // DC


def chunks_of(f):
    return range(CHUNK0[f], CHUNK0[f] + LOOKUP[f] // LR)


def row_numbers(np):
    return np.concatenate([np.arange(rows).reshape(LR, rows // LR) for rows in LOOKUP.values()], 1).astype(np.int32)


def weight_scale(np):
    w = np.zeros((P, NS), np.float32)
    w[:, S_XY:S_1] = 1.0
    w[(X - NG) * NF:, S_G] = 0.0
    w[0, S_1 + 1:S_1 + N1] = 1.0
    for c, l, _, _, hi in SEG_IN:
        lo = next(a for a, b in GROUPS if b == hi)
        for m in range(l, hi):
            r = c - LO1 + m - l
            w[r, S_1] = 0.5 if l == m else 1.0
            for j in range(F):
                if not lo <= j < m:
                    w[r, S_1 + 1 + j] = 1.0 / {1: 6, 2: 2, 3: 1}[len({l, m, j})]
    return w


def dlrm_program(nc, ids, ids_lookup, rows, tables, dense_t, w1, w2t, b1, b2, wt1, bt1, wt2, bt2, wt3, scale, ident,
                 out):
    with ExitStack() as ctx:
        def sb(name, shape, dt=F32):
            return ctx.enter_context(nc.sbuf_tensor(name + "_sb", shape, dt))

        def sem(name):
            return ctx.enter_context(nc.semaphore(name))

        bank = ctx.enter_context(nc.psum_tensor("bank", [P, 8, 512], F32))
        T_BANK = (0, 1)
        HALF_BANK = (2, 3)
        TOP_BANK = (4, 5)
        LOOKUP_BANK = 6
        Z_BANK = 7
        T = sb("sums", [P, NS, BLK])
        GS = sb("gram", [P, X, P])
        SP = T[:, :, P:P + P]
        Q_W = NQ * K
        shared = sb("shared", [P, max(F * V1W, Q_W + NS * H)])
        V1 = shared[:, 0:F * V1W].rearrange("p (j x) -> p j x", x=V1W)
        V = shared[:, Q_W:Q_W + NS * H].rearrange("p (s h) -> p s h", h=H)
        Q = [sb("products0", [P, NQ, K])[:], shared[:, 0:Q_W].rearrange("p (c b) -> p c b", b=K)]
        BD = [sb(f"blockdiag{u}", [P, K, Q4, N1]) for u in range(2)]
        E = [sb(f"embedding{u}", [P, F * K]) for u in range(2)]
        idx_all = sb("idx_all", [P, NB // P, F], I32)
        idx = [sb(f"idx{u}", [P, F], I32) for u in range(2)]
        w1_sb = sb("w1", [P, F, F])
        w1s = sb("w1_sym", [P, V1W])
        w2_sb = sb("w2", [P, F, H])
        scale_sb = sb("scale", [P, NS])
        ident_sb = sb("ident", [P, P])
        b_sb = sb("cin_bias", [P, 2])
        bk_sb = sb("cin_bias_k", [P, 2])
        dense_parts = sb("dense_parts", [len(DPARTS) * DC, NB], BF16)
        wt1d_parts = sb("w_top1_dense_parts", [len(WPARTS) * DC, D1], BF16)
        wt1_sb = sb("w_top1", [P, 2, D1])
        bt1_sb = sb("b_top1", [P, D1 // P])
        wt2_sb = sb("w_top2", [P, D1 // P, D2])
        bt2_sb = sb("b_top2", [P, D2 // P])
        wt3_sb = sb("w_top3", [P, D2 // P])
        ones_sb = sb("ones", [P, 1])
        M1, M2 = D1 // P, D2 // P
        top = sb("top_activations", [P, 2 + M1 + M2, BLK])
        z_sb, h1_sb, h2_sb = top[:, 0:2], top[:, 2:2 + M1], top[:, 2 + M1:2 + M1 + M2]
        y_sb = sb("y", [1, BLK])
        rows_sb = sb("row_numbers", [LR, LCH], I32)
        table_parts = sb("table_parts", [LR, LCH, PARTS, K], BF16)
        ids_sb = [sb(f"lookup_ids{u}", [LR, NL, P], I32) for u in range(2)]
        one_hot = sb("one_hot", [LR, LCH, P], BF16)
        early = top[:].rearrange("p c b -> p (c b)")
        table_f32 = early[0:LR, 0:LCH * K].rearrange("p (c k) -> p c k", k=K)
        WD, WW = NB // DG, D1 // DG
        at = LCH * K
        dense_f32 = early[:, at:at + WD + WW]
        dense_part = [early[:, a:a + (WD + WW) // 2].bitcast(BF16)
                      for a in range(at + WD + WW, at + (WD + WW) * 5 // 2, (WD + WW) // 2)]

        W2_PARTS = ((0, 2), (2, 8), (8, F))
        s_ids = sem("ids_loaded")
        s_w1load = sem("w1_loaded")
        s_w2load = [sem(f"w2_loaded{n}") for n in range(len(W2_PARTS))]
        s_cload = sem("constants_loaded")
        s_tload = sem("top_weights_loaded")
        s_zero = sem("blockdiag_zeroed")
        s_dload = sem("dense_loaded")
        s_lids = [sem(f"lookup_ids_loaded{u}") for u in range(2)]
        s_hot = sem("one_hot_ready")
        s_look = sem("lookup_ready")
        s_lrow = sem("lookup_rows_copied")
        s_cast = sem("dense_part_rounded")
        s_rest = sem("dense_rest_ready")
        s_parts = sem("dense_parts_spread")
        s_w1s = sem("w1_sym_ready")
        s_v1 = sem("v1_products_ready")
        s_v1c = [sem("v1_copied_by_act"), sem("v1_copied_by_dve")]
        s_add = sem("weight_sums_step")
        s_addp = sem("weight_sums_gpsimd_step")
        s_vt = sem("weights_transposed")
        s_v = sem("weights_scaled")
        s_bk = sem("cin_bias_ready")
        s_idx = [sem(f"tile_indices_copied{u}") for u in range(2)]
        s_emb = [[sem(f"embeddings_gathered{u}_{n}") for n in range(3)] for u in range(2)]
        s_et = [sem(f"embeddings_transposed{u}") for u in range(2)]
        s_q0 = [sem(f"rows0_operands_ready{u}") for u in range(2)]
        s_q1 = [sem(f"rows1_operands_ready{u}") for u in range(2)]
        s_p0 = sem("octet_rows0_ready")
        s_p1 = [sem(f"half_rows1_ready{u}") for u in range(2)]
        s_e0 = [sem(f"rows0_copied{r}") for r in range(2)]
        s_e1 = [sem(f"rows1_copied{k}") for k in range(2)]
        s_gab = sem("gram_ab_moved")
        s_z = sem("z_ready")
        s_zc = sem("z_copied")
        s_h1 = sem("h1_ready")
        s_h1c = sem("h1_copied")
        s_h2 = sem("h2_ready")
        s_h2c = sem("h2_copied")
        s_fold = sem("h2_weighted_step")
        s_y = sem("y_ready")
        s_yc = sem("y_copied")
        s_out = sem("y_stored")

        FREE = 1
        HALVES = 2 * OCT
        SLABS = [*range(S_XYC, S_G), *range(S_1 + 1, NS), S_1, S_XY, S_G]
        Z2_SLABS = NS - 3
        QUADS = -(-NS // 4)
        W_BANKS = 6
        COLS = (slice(0, P), slice(P, BLK))

        def pairs(t, j0, j1, l0, l1, m0, m1):
            lo = min(l0, m0)
            at, first, rows = ((V1_C, C, X), (V1_X, X, Y - X), (V1_Y, Y, F - Y))[(lo >= X) + (lo >= Y)]
            width = F - first
            v = t[:, :, at:at + rows * width].rearrange("p j (l m) -> p j l m", m=width)
            if l1 <= first + rows and m0 >= first:
                return v[:, j0:j1, l0 - first:l1 - first, m0 - first:m1 - first]
            assert m1 <= first + rows and l0 >= first
            return v[:, j0:j1, m0 - first:m1 - first, l0 - first:l1 - first].rearrange("p j m l -> p j l m")

        def target(s0, c0, j0, j1, seg):
            c, l0, l1, m0, m1 = seg
            n = (l1 - l0) * (m1 - m0)
            return SP[:, s0 + j0:s0 + j1, c - c0:c - c0 + n].rearrange("p j (l m) -> p j l m", l=l1 - l0)

        def sum_weights(engine, parts, step):
            for s0, c0, j0, j1, seg in parts:
                _, l0, l1, m0, m1 = seg
                to = target(s0, c0, j0, j1, seg)
                if step == 0:
                    ins = engine.tensor_tensor(to, pairs(V1, j0, j1, l0, l1, m0, m1),
                                               pairs(V1, m0, m1, l0, l1, j0, j1).rearrange("p m l j -> p j l m"),
                                               ALU.add)
                else:
                    ins = engine.tensor_tensor(to, to,
                                               pairs(V1, l0, l1, m0, m1, j0, j1).rearrange("p l m j -> p j l m"),
                                               ALU.add)
            return ins

        PARTS_POOL = [(S_XYC - h * XH, -h * XYR, h * XH, (h + 1) * XH, seg) for h in range(2) for seg in SEG_XY]
        PARTS_DVE = []
        for seg in SEG_IN:
            cuts = (C, F) if seg[1] < X else (C, X, F) if seg[1] < Y else (C, X, Y, F)
            PARTS_DVE += [(S_1 + 1, LO1, j0, j1, seg) for j0, j1 in zip(cuts, cuts[1:])]
        V1_DVE = range(1, 9, 2)
        V1_ACT = [j for j in range(F) if j not in V1_DVE]

        def v1_copied(engine, j):
            mine = V1_DVE if j in V1_DVE else V1_ACT
            engine.wait_ge(s_v1c[mine is V1_DVE], list(mine).index(j) + 1)

        def v1_complete(engine):
            engine.wait_ge(s_v1c[0], len(V1_ACT))
            engine.wait_ge(s_v1c[1], len(V1_DVE))

        def gathered(lo, hi):
            return [f for f in range(lo, hi) if f not in LOOKUP]

        block = ctx.enter_context(nc.Block())

        @block.sync
        def _(sp):
            sp.dma_start(w1_sb[:], w1).then_inc(s_w1load, 16)
            for n, (lo, hi) in enumerate(W2_PARTS):
                sp.dma_start(w2_sb[:, lo:hi, :], w2t[:, lo:hi, :]).then_inc(s_w2load[n], 16)

            def load_lookup_ids(t, u):
                sp.dma_start(ids_sb[u][:], ids_lookup[:, bass.ds(P * t, P)].unsqueeze(0).broadcast_to([LR, NL, P])
                             ).then_inc(s_lids[u], 16)

            load_lookup_ids(0, 0)
            sp.dma_start(rows_sb[:], rows).then_inc(s_dload, 16)
            for f in LOOKUP:
                sp.dma_start(table_f32[:, chunks_of(f)[0]:chunks_of(f)[-1] + 1],
                             tables[f].rearrange("(p c) k -> p c k", p=LR)).then_inc(s_dload, 16)
            sp.dma_start(dense_f32[:, 0:WD], dense_t.rearrange("d (g b) -> (d g) b", g=DG)).then_inc(s_dload, 16)
            sp.dma_start(dense_f32[:, WD:WD + WW],
                         wt1[2 * H:2 * H + DC].rearrange("d (g n) -> (d g) n", g=DG)).then_inc(s_dload, 16)
            load_lookup_ids(1, 1)
            for dst, src in ((scale_sb[:], scale), (ident_sb[:], ident), (b_sb[:, 0:1], b1), (b_sb[:, 1:2], b2)):
                sp.dma_start(dst, src).then_inc(s_cload, 16)
            for dst, src in ((wt1_sb[:], wt1[0:2 * H].rearrange("(c p) n -> p c n", p=P)),
                             (wt2_sb[:], wt2.rearrange("(c p) n -> p c n", p=P)),
                             (bt1_sb[:], bt1), (bt2_sb[:], bt2), (wt3_sb[:], wt3)):
                sp.dma_start(dst, src).then_inc(s_tload, 16)

            for k, part in enumerate("hml"):
                sp.wait_ge(s_cast, 2 * k + 2)
                for parts, dst, cols in ((DPARTS, dense_parts, slice(0, WD)),
                                         (WPARTS, wt1d_parts, slice(WD, WD + WW))):
                    for n in range(len(parts)):
                        if parts[n] == part:
                            sp.dma_start(dst[n * DC:(n + 1) * DC, :].rearrange("d (g b) -> d g b", g=DG),
                                         dense_part[k][:, cols]
                                         ).then_inc(s_parts, 16)

            y_tiles = out.rearrange("(t b) o -> t o b", b=P)

            def spread_gram(t, u):
                for r in range(2):
                    sp.wait_ge(s_e0[r], OCT // 2 * (t + 1) + FREE)
                for j in range(X):
                    s, r = (S_G, j * NF) if j < X - NG else (S_XY, XYR + (j - X + NG) * NF)
                    sp.dma_start(T[r:r + NF, s, COLS[u]], GS[XYR:R0, j, :]).then_inc(s_gab, 16)

            def store(t, u):
                sp.wait_ge(s_yc, t + 1)
                sp.dma_start(y_tiles[t], y_sb[:, COLS[u]]).then_inc(s_out, 16)

            def tile(g, u, last=False):
                t = 2 * g + u
                if not last:
                    sp.wait_ge(s_hot, NL * t)
                    load_lookup_ids(t + 1, 1 - u)
                spread_gram(t, u)
                store(t - 1, 1 - u)

            spread_gram(0, 0)
            tile(0, 1)
            with sp.Fori(1, BLOCKS - 1) as g:
                tile(g, 0)
                tile(g, 1)
            tile(BLOCKS - 1, 0)
            tile(BLOCKS - 1, 1, last=True)
            store(TILES - 1, 1)
            sp.wait_ge(s_out, 16 * (TILES + FREE))

        @block.gpsimd
        def _(pool):
            pool.wait_ge(s_ids, 16)

            def gather(g, u):
                pool.wait_ge(s_et[u], 3 * g + FREE)
                pool.tensor_copy(idx[u][:], idx_all[:, 2 * g + u, :]).then_inc(s_idx[u], 1)
                pool.wait_ge(s_idx[u], g + 1)
                pool.nop(nofuse=True)
                for n, (lo, hi) in enumerate(ARRIVAL):
                    for f in gathered(lo, hi):
                        pool.indirect_dma_start(
                            out=E[u][:, f * K:(f + 1) * K], out_offset=None, in_=tables[f],
                            in_offset=bass.IndirectOffsetOnAxis(ap=idx[u][:, f:f + 1].bitcast(U32), axis=0),
                        ).then_inc(s_emb[u][n], 16)

            gather(0, 0)
            v1_complete(pool)
            pool.wait_ge(s_add, 1)
            sum_weights(pool, PARTS_POOL, 0).then_inc(s_addp, 1)
            pool.wait_ge(s_addp, 1)
            sum_weights(pool, PARTS_POOL, 1).then_inc(s_addp, 1)
            gather(0, 1)
            with pool.Fori(1, BLOCKS) as g:
                gather(g, 0)
                gather(g, 1)

        @block.tensor
        def _(pe):
            for u in range(2):
                pe.sem_inc(s_p1[u], FREE)
            pe.wait_ge(s_w1load, 32)
            pe.wait_ge(s_w1s, 1)
            for j in range(F):
                for n, (lo, _) in enumerate(W2_PARTS):
                    if j == lo:
                        pe.wait_ge(s_w2load[n], 16)
                if j >= 8:
                    v1_copied(pe, j - 8)
                pe.matmul(bank[:, j % 8, 0:V1W], w2_sb[:, j, :], w1s[:], start=True, stop=True).then_inc(s_v1, 1)
            v1_complete(pe)

            def weight_transposes():
                pe.wait_ge(s_add, 4)
                pe.wait_ge(s_addp, 2)
                pe.wait_ge(s_cload, 16 * 4)
                for k in range(2):
                    pe.wait_ge(s_e0[k], OCT // 2 + FREE)
                    pe.wait_ge(s_e1[k], OCT + FREE)
                for i in range(QUADS):
                    if i >= W_BANKS:
                        pe.wait_ge(s_v, 4 * (i - W_BANKS + 1))
                    for n, s in enumerate(SLABS[4 * i:4 * i + 4]):
                        mm = pe.transpose(bank[:, i % W_BANKS, n * H:(n + 1) * H], SP[:, s, :], ident_sb[:])
                    mm.then_inc(s_vt, 1)

            def rows0_sums(g, u, t, octets):
                if octets[0] == 0:
                    pe.wait_ge(s_q0[u], g + 1)
                for o in octets:
                    r = o % 2
                    pe.wait_ge(s_e0[r], OCT // 2 * t + o // 2 + FREE)
                    for b in range(8):
                        mm = pe.matmul(bank[0:R0, T_BANK[r], b * Q4 * N0:(b + 1) * Q4 * N0],
                                       Q[u][:, 0:R0, 8 * o + b], BD[u][:, 8 * o + b, :, 0:N0],
                                       start=True, stop=True)
                    mm.then_inc(s_p0, 1)

            def rows1_sums(g, u, t, octets):
                if octets[0] == 0:
                    pe.wait_ge(s_q1[u], g + 1)
                for o in octets:
                    for k in range(2):
                        pe.wait_ge(s_e1[k], OCT * t + o + FREE)
                        for b in range(4):
                            mm = pe.matmul(bank[0:R1, HALF_BANK[k], b * Q4 * N1:(b + 1) * Q4 * N1],
                                           Q[u][:, LO1:HI1, 8 * o + 4 * k + b],
                                           BD[u][:, 8 * o + 4 * k + b, :, 0:N1], start=True, stop=True)
                        mm.then_inc(s_p1[u], 1)

            def lookup(t, first=False):
                if not first:
                    pe.wait_ge(s_lrow, t)
                for i, f in enumerate(LOOKUP):
                    pe.wait_ge(s_hot, NL * t + i + 1)
                    for c in chunks_of(f):
                        mm = pe.matmul(bank[:, LOOKUP_BANK, i * PARTS * K:(i + 1) * PARTS * K], one_hot[:, c, :],
                                       table_parts[:, c].rearrange("p s k -> p (s k)"),
                                       start=(c == chunks_of(f)[0]), stop=(c == chunks_of(f)[-1]))
                mm.then_inc(s_look, 1)

            def z_sums(t, u, first=False):
                z1, z2 = (bank[:, Z_BANK, k * P:(k + 1) * P] for k in range(2))
                pe.wait_ge(s_zc, 2 * t + FREE)
                for r in range(2):
                    pe.wait_ge(s_e0[r], OCT // 2 * (t + 1) + FREE)
                for k in range(2):
                    pe.wait_ge(s_e1[k], OCT * (t + 1) + FREE)
                for n, s in enumerate(SLABS):
                    if first and n % 4 == 0:
                        pe.wait_ge(s_v, min(n + 4, NS))
                    if s == S_XY:
                        pe.wait_ge(s_gab, 16 * X * (t + 1))
                    z = z2 if n < Z2_SLABS else z1
                    rows = slice(0, (X - NG) * NF if s == S_G else P if s < S_G else R1)
                    mm = pe.matmul(z, V[rows, s, :], T[rows, s, COLS[u]], start=n in (0, Z2_SLABS),
                                   stop=n in (Z2_SLABS - 1, NS - 1))
                mm.then_inc(s_z, 1)

            def top1(t, u, chunks, first=False):
                if chunks[0] == 0:
                    if not first:
                        pe.wait_ge(s_yc, t)
                    pe.wait_ge(s_zc, 2 * (t + 1) + FREE)
                for c in chunks:
                    n = slice(c * P, (c + 1) * P)
                    h = bank[:, TOP_BANK[c % 2], 0:P]
                    if c >= 2:
                        pe.wait_ge(s_h1c, M1 * t + c - 1)
                    pe.matmul(h, wt1_sb[:, 0, n], z_sb[:, 0, COLS[u]], start=True, stop=False)
                    pe.matmul(h, wt1_sb[:, 1, n], z_sb[:, 1, COLS[u]], start=False, stop=False)
                    pe.matmul(h, wt1d_parts[:, n], dense_parts[:, bass.ds(P * t, P)],
                              start=False, stop=True).then_inc(s_h1, 1)

            def top2(t, u):
                pe.wait_ge(s_h1c, M1 * (t + 1))
                for c in range(M2):
                    for k in range(M1):
                        mm = pe.matmul(bank[:, TOP_BANK[c], 0:P], wt2_sb[:, k, c * P:(c + 1) * P],
                                       h1_sb[:, k, COLS[u]], start=(k == 0), stop=(k == M1 - 1))
                    mm.then_inc(s_h2, 1)

            def top3(t, u):
                pe.wait_ge(s_fold, M2 * (t + 1))
                pe.matmul(bank[0:1, TOP_BANK[0], 0:P], ones_sb[:], h2_sb[:, 0, COLS[u]],
                          start=True, stop=True).then_inc(s_y, 1)

            def tile(g, u, first=False, last=False):
                t = 2 * g + u
                rows0_sums(g, u, t, (0, 1))
                top1(t - 1, 1 - u, (0, 1), first)
                rows0_sums(g, u, t, (2,))
                top1(t - 1, 1 - u, (2, 3))
                rows0_sums(g, u, t, (3,))
                rows1_sums(g, u, t, (0, 1))
                top2(t - 1, 1 - u)
                rows1_sums(g, u, t, (2, 3))
                if not last:
                    lookup(t + 1)
                top3(t - 1, 1 - u)
                z_sums(t, u)

            pe.wait_ge(s_cast, 6)
            lookup(0, first=True)
            rows0_sums(0, 0, 0, range(OCT))
            rows1_sums(0, 0, 0, range(OCT))
            lookup(1)
            weight_transposes()
            z_sums(0, 0, first=True)
            pe.wait_ge(s_tload, 16 * 5)
            pe.wait_ge(s_parts, 16 * 2 * len(DPARTS))
            tile(0, 1, first=True)
            with pe.Fori(1, BLOCKS - 1) as g:
                tile(g, 0)
                tile(g, 1)
            tile(BLOCKS - 1, 0)
            tile(BLOCKS - 1, 1, last=True)
            top1(TILES - 1, 1, range(M1))
            top2(TILES - 1, 1)
            top3(TILES - 1, 1)

        @block.scalar
        def _(act):
            act.dma_start(idx_all[:], ids.rearrange("(t p) f -> p t f", p=P)).then_inc(s_ids, 16)
            act.dma_start(w1s[:, V1W - 1:V1W], b1).then_inc(s_w1load, 16)

            def round_parts(n):
                if n == 0:
                    act.wait_ge(s_dload, 16 * (3 + NL))
                else:
                    act.wait_ge(s_rest, 2 * n)
                act.activation(dense_part[n], dense_f32, ACT.Copy).then_inc(s_cast, 1)
                act.activation(table_parts[:, :, n, :], table_f32, ACT.Copy).then_inc(s_cast, 1)

            act.sem_inc(s_out, 16 * FREE)
            act.sem_inc(s_zc, FREE)
            for r in range(2):
                act.sem_inc(s_e0[r], FREE)
                act.sem_inc(s_e1[r], FREE)
            for u in range(2):
                ins = act.memzero(BD[u][:])
            ins.then_inc(s_zero, 1)
            for j in V1_ACT:
                act.wait_ge(s_v1, j + 1)
                act.activation(V1[:, j, :], bank[:, j % 8, 0:V1W], ACT.Copy).then_inc(s_v1c[0], 1)
                if j in (6, 10, 14):
                    round_parts(j // 4 - 1)
            To = T[:].rearrange("p j (u q o b) -> p u o j q b", u=2, q=Q4, o=OCT)
            GSo = GS[:].rearrange("p j (q o b) -> p o j q b", q=Q4, o=OCT)
            T1o = T[:, S_1:NS].rearrange("p j (u q o k b) -> p u o k j q b", u=2, q=Q4, o=OCT, k=2)

            def copy_rows0(t, u, octets, first=False):
                if octets[0] == 0 and not first:
                    act.wait_ge(s_gab, 16 * X * t)
                for o in octets:
                    r = o % 2
                    act.wait_ge(s_p0, OCT * t + o + 1)
                    sums = bank[:, T_BANK[r], 0:8 * Q4 * N0].rearrange("p (b q j) -> p j q b", b=8, q=Q4)
                    act.activation(To[0:XYR, u, o, S_XY:S_G], sums[0:XYR, 0:1 + XH], ACT.Copy)
                    act.activation(To[XYR:P, u, o, S_XYC:S_G], sums[0:XYR, 1 + XH:N0], ACT.Copy)
                    act.activation(GSo[XYR:R0, o], sums[XYR:R0, 1:N0], ACT.Copy).then_inc(s_e0[r], 1)

            def copy_rows1(g, u, octets):
                for o in octets:
                    for k in range(2):
                        act.wait_ge(s_p1[u], HALVES * g + 2 * o + k + 1 + FREE)
                        act.activation(T1o[0:R1, u, o, k],
                                       bank[0:R1, HALF_BANK[k], 0:4 * Q4 * N1].rearrange(
                                           "p (b q j) -> p j q b", b=4, q=Q4),
                                       ACT.Copy).then_inc(s_e1[k], 1)

            def copy_z(t, u):
                act.wait_ge(s_z, t + 1)
                for k in range(2):
                    act.activation(z_sb[:, k, COLS[u]], bank[:, Z_BANK, k * P:(k + 1) * P], ACT.Identity,
                                   bias=bk_sb[:, k:k + 1]).then_inc(s_zc, 1)

            def copy_h1(t, u, chunks):
                for c in chunks:
                    act.wait_ge(s_h1, M1 * t + c + 1)
                    act.activation(h1_sb[:, c, COLS[u]], bank[:, TOP_BANK[c % 2], 0:P], ACT.Relu,
                                   bias=bt1_sb[:, c:c + 1]).then_inc(s_h1c, 1)

            def copy_h2(t, u):
                for c in range(M2):
                    act.wait_ge(s_h2, M2 * t + c + 1)
                    act.activation(h2_sb[:, c, COLS[u]], bank[:, TOP_BANK[c], 0:P], ACT.Relu,
                                   bias=bt2_sb[:, c:c + 1]).then_inc(s_h2c, 1)

            def copy_y(t, u):
                act.wait_ge(s_out, 16 * (t + FREE))
                act.wait_ge(s_y, t + 1)
                act.activation(y_sb[:, COLS[u]], bank[0:1, TOP_BANK[0], 0:P], ACT.Copy).then_inc(s_yc, 1)

            def tile(g, u):
                t = 2 * g + u
                copy_rows0(t, u, (0, 1))
                copy_h1(t - 1, 1 - u, (0, 1))
                copy_rows0(t, u, (2,))
                copy_h1(t - 1, 1 - u, (2, 3))
                copy_rows0(t, u, (3,))
                copy_rows1(g, u, (0, 1))
                copy_h2(t - 1, 1 - u)
                copy_rows1(g, u, (2, 3))
                copy_y(t - 1, 1 - u)
                copy_z(t, u)

            copy_rows0(0, 0, range(OCT), first=True)
            copy_rows1(0, 0, range(OCT))
            act.wait_ge(s_add, 4)
            act.wait_ge(s_addp, 2)
            act.wait_ge(s_cload, 16 * 4)
            for i, s in enumerate(SLABS):
                if i % 4 == 0:
                    act.wait_ge(s_vt, i // 4 + 1)
                act.activation(V[:, s, :], bank[:, i // 4 % W_BANKS, i % 4 * H:(i % 4 + 1) * H], ACT.Copy,
                               scale=scale_sb[:, s:s + 1]).then_inc(s_v, 1)
            act.wait_ge(s_tload, 16 * 5)
            act.mul(bk_sb[:], b_sb[:], float(K)).then_inc(s_bk, 1)
            act.wait_ge(s_bk, 1)
            act.wait_ge(s_parts, 16 * 2 * len(DPARTS))
            copy_z(0, 0)
            tile(0, 1)
            with act.Fori(1, BLOCKS) as g:
                tile(g, 0)
                tile(g, 1)
            copy_h1(TILES - 1, 1, range(M1))
            copy_h2(TILES - 1, 1)
            copy_y(TILES - 1, 1)

        @block.vector
        def _(dve):
            for u in range(2):
                dve.sem_inc(s_et[u], FREE)

            def less_part(n):
                dve.wait_ge(s_cast, 2 * n + 2)
                for rest, part in ((dense_f32, dense_part[n]), (table_f32, table_parts[:, :, n, :])):
                    dve.tensor_tensor(rest, rest, part, ALU.subtract).then_inc(s_rest, 1)

            def one_hot_columns(g, u, f):
                i, n = list(LOOKUP).index(f), len(chunks_of(f))
                chunks = slice(CHUNK0[f], CHUNK0[f] + n)
                dve.wait_ge(s_lids[u], 16 * (g + 1))
                dve.tensor_tensor(one_hot[:, chunks, :], ids_sb[u][:, i:i + 1, :].broadcast_to([LR, n, P]),
                                  rows_sb[:, chunks].unsqueeze(2).broadcast_to([LR, n, P]),
                                  ALU.is_equal).then_inc(s_hot, 1)

            def lookup_columns(g, u):
                dve.wait_ge(s_look, 2 * g + u)
                for f in LOOKUP:
                    one_hot_columns(g, u, f)

            def group_operands(g, u, n):
                lo, hi = ARRIVAL[n]
                if n == 0:
                    dve.wait_ge(s_p1[u], HALVES * g + FREE)
                if lo == C:
                    dve.wait_ge(s_look, 2 * g + u + 1)
                    for i, f in enumerate(LOOKUP):
                        ins = dve.tensor_reduce(
                            E[u][:, f * K:(f + 1) * K],
                            bank[:, LOOKUP_BANK, i * PARTS * K:(i + 1) * PARTS * K].rearrange("p (s k) -> p k s", k=K),
                            mybir.AxisListType.X, ALU.add)
                    ins.then_inc(s_lrow, 1)
                    dve.wait_ge(s_lrow, 2 * g + u + 1)
                dve.wait_ge(s_emb[u][n], 16 * len(gathered(lo, hi)) * (g + 1))
                dve.transpose(Q[u][:, field_columns(lo, hi), :].rearrange("p i b -> p (i b)"),
                              E[u][:, lo * K:hi * K]).then_inc(s_et[u], 1)
                dve.wait_ge(s_et[u], 3 * g + n + 1 + FREE)
                for q in range(Q4):
                    rows = slice(q * K, (q + 1) * K)
                    ins = dve.tensor_copy(BD[u][rows, :, q, 1 + lo:1 + hi],
                                          Q[u][rows, field_columns(lo, hi), :].rearrange("p i b -> p b i"))
                if n == 2:
                    ins.then_inc(s_q0[u], 1)
                segs = ([seg for seg in SEG_IN if seg[4] == Y], SEG_XY, [seg for seg in SEG_IN if seg[4] != Y])[n]
                for c, l0, l1, m0, m1 in segs:
                    L, M = l1 - l0, m1 - m0
                    ins = dve.tensor_tensor(
                        Q[u][:, c:c + L * M, :].rearrange("p (l m) b -> p l m b", l=L),
                        Q[u][:, field_columns(l0, l1), :].unsqueeze(2).broadcast_to([P, L, M, K]),
                        Q[u][:, field_columns(m0, m1), :].unsqueeze(1).broadcast_to([P, L, M, K]), ALU.mult)
                if n == 2:
                    ins.then_inc(s_q1[u], 1)

            def weight_h2(t, u):
                dve.wait_ge(s_h2c, M2 * (t + 1))
                sums = h2_sb[:, 0, COLS[u]]
                dve.tensor_scalar(sums, sums, wt3_sb[:, 0:1], None, ALU.mult).then_inc(s_fold, 1)
                for k in range(1, M2):
                    dve.wait_ge(s_fold, M2 * t + k)
                    dve.scalar_tensor_tensor(sums, h2_sb[:, k, COLS[u]], wt3_sb[:, k:k + 1], sums, ALU.mult,
                                             ALU.add).then_inc(s_fold, 1)

            def tile_operands(g, u, first=False):
                group_operands(g, u, 0)
                if not first:
                    weight_h2(2 * g + u - 2, u)
                group_operands(g, u, 1)
                group_operands(g, u, 2)

            ZEROED = NS * 3 // 4
            dve.memset(SP[:, 0:ZEROED], 0.0)
            dve.memset(ones_sb[:], 1.0)
            w1v = w1s[:].unsqueeze(1)
            turned = w1_sb[:].rearrange("p m l -> p l m")
            dve.wait_ge(s_w1load, 32)
            for l0, l1 in GROUPS:
                ins = dve.tensor_tensor(pairs(w1v, 0, 1, l0, l1, l0, F).squeeze(1), w1_sb[:, l0:l1, l0:F],
                                        turned[:, l0:l1, l0:F], ALU.add)
            ins.then_inc(s_w1s, 1)
            dve.memset(SP[:, ZEROED:NS], 0.0).then_inc(s_add, 1)
            dve.memset(Q[0][:, C_ONE, :], 1.0)
            dve.wait_ge(s_add, 1)
            dve.wait_ge(s_w1s, 1)
            for s, c0, segs in ((S_XY, 0, SEG_XY), (S_1, LO1, SEG_IN)):
                for c, l0, l1, m0, m1 in segs:
                    n = (l1 - l0) * (m1 - m0)
                    dve.tensor_copy(SP[:, s:s + 1, c - c0:c - c0 + n].rearrange("p s (l m) -> p s l m", l=l1 - l0),
                                    pairs(w1v, 0, 1, l0, l1, m0, m1))
            for s, r, ja, jb in ((S_G, 0, 0, X - NG), (S_XY, XYR, X - NG, X)):
                dve.tensor_copy(
                    SP[:, s:s + 1, r:r + (jb - ja) * NF].rearrange("p s (j i) -> p s j i", i=NF),
                    pairs(w1v, 0, 1, ja, jb, X, F))
            dve.wait_ge(s_zero, 1)
            for u in range(2):
                for q in range(Q4):
                    dve.memset(BD[u][q * K:(q + 1) * K, :, q, 0:1], 1.0)
            for j in V1_DVE:
                dve.wait_ge(s_v1, j + 1)
                dve.tensor_copy(V1[:, j, :], bank[:, j % 8, 0:V1W]).then_inc(s_v1c[1], 1)
            for n, f in enumerate(LOOKUP):
                if n < PARTS - 1:
                    less_part(n)
                one_hot_columns(0, 0, f)
            group_operands(0, 0, 0)
            group_operands(0, 0, 1)
            v1_complete(dve)
            dve.wait_ge(s_add, 1)
            EARLY = 8
            sum_weights(dve, PARTS_DVE[:EARLY], 0)
            group_operands(0, 0, 2)
            sum_weights(dve, PARTS_DVE[EARLY:], 0).then_inc(s_add, 1)
            dve.wait_ge(s_add, 2)
            sum_weights(dve, PARTS_DVE, 1).then_inc(s_add, 1)
            dve.tensor_copy(SP[:, S_1 + 1:S_1 + 1 + F, C_ONE - LO1], V1[:, :, V1_U]).then_inc(s_add, 1)
            dve.wait_ge(s_add, 4)
            dve.wait_ge(s_addp, 2)
            dve.memset(Q[1][:, C_ONE, :], 1.0)
            lookup_columns(0, 1)
            tile_operands(0, 1, first=True)
            with dve.Fori(1, BLOCKS) as g:
                for u in range(2):
                    lookup_columns(g, u)
                    tile_operands(g, u)
            weight_h2(TILES - 2, 0)
            weight_h2(TILES - 1, 1)


def kernel(**inputs):
    import numpy as np
    import concourse.bacc as bacc
    from concourse import mybir
    from concourse.bass_utils import run_bass_kernel_spmd as run

    nc = bacc.Bacc("TRN2", target_bir_lowering=False, num_devices=1)
    arrays = {}

    def given(name, a):
        arrays[name] = np.ascontiguousarray(a)
        return nc.dram_tensor(name, arrays[name].shape, mybir.dt.from_np(arrays[name].dtype),
                              kind="ExternalInput").ap()

    args = [
        given("ids", inputs["ids"]),
        given("ids_lookup", np.asarray(inputs["ids"]).T[list(LOOKUP)]),
        given("row_number", row_numbers(np)),
        [given(f"tbl_{f}", inputs[f"tbl_{f}"]) for f in range(F)],
        given("dense_t", np.asarray(inputs["dense_ctx"]).T),
        given("w1", inputs["L0_rec_W1"]),
        given("w2t", np.asarray(inputs["L0_rec_W2"]).transpose(1, 2, 0)),
        given("b1", np.asarray(inputs["L0_rec_b1"]).reshape(H, 1)),
        given("b2", np.asarray(inputs["L0_rec_b2"]).reshape(H, 1)),
        given("w_top1_in", inputs["W_top1"]),
        given("b_top1_in", np.asarray(inputs["b_top1"]).reshape(D1 // P, P).T),
        given("w_top2_in", inputs["W_top2"]),
        given("b_top2_in", np.asarray(inputs["b_top2"]).reshape(D2 // P, P).T),
        given("w_top3_in", np.asarray(inputs["W_top3"]).reshape(D2 // P, P).T),
        given("weight_scale", weight_scale(np)),
        given("identity", np.eye(P, dtype=np.float32)),
    ]
    out = nc.dram_tensor("y_out", (NB, 1), F32, kind="ExternalOutput").ap()
    dlrm_program(nc, *args, out)
    return run(nc, [arrays], core_ids=[0]).results[0]["y_out"]
```
